# Optimizing a Trainium2 kernel written in Bass

```python
import numpy as np
import jax
import jax.numpy as jnp

def _softmax(x, axis=-1):
    return jax.nn.softmax(x, axis=axis)

def _gelu(x):
    return jax.nn.gelu(x, approximate=True)

def _silu(x):
    return jax.nn.silu(x)

def _sigmoid(x):
    return jax.nn.sigmoid(x)

def _layernorm(x, axis=-1, eps=1e-05):
    m = jnp.mean(x, axis=axis, keepdims=True)
    v = jnp.var(x, axis=axis, keepdims=True)
    return (x - m) / jnp.sqrt(v + eps)

def _scatter_add(tgt, idx, src, axis=0):
    return tgt.at[idx].add(src)

def _segment_sum(src, seg, n):
    return jax.ops.segment_sum(src, seg, n)
kernel_name = 'mk_decoder_preln_d1_seqx_r8_36881b'

def setup_inputs(seed: int=0):
    np.random.seed(seed)
    _w = jnp.asarray

    def _rec_inputs():
        import jax
        import jax.numpy as jnp
        _rk = jax.random.key(seed)
        x = 0.0002417 + 0.9998 * jax.random.normal(jax.random.fold_in(_rk, 1), (8, 128, 128), jnp.float32)
        _lenS = 128 - jax.random.randint(jax.random.fold_in(_rk, 7), (8,), 0, max(1, 128 // 4) + 1, jnp.int32)
        _lenS2 = 77 - jax.random.randint(jax.random.fold_in(_rk, 8), (8,), 0, max(1, 77 // 4) + 1, jnp.int32)
        _ctx_1024P = jax.random.normal(jax.random.fold_in(_rk, 11), (8, 16, 128), jnp.float32)
        _ctx_1024c = jax.random.dirichlet(jax.random.fold_in(_rk, 511), 0.3 * jnp.ones((16,), jnp.float32), (8, 77))
        _ctx_1024t = jnp.einsum('bsk,bkd->bsd', _ctx_1024c, _ctx_1024P)
        _ctx_1024t = _ctx_1024t * jax.lax.rsqrt(jnp.mean(jnp.square(_ctx_1024t)) + 1e-12) * 0.953939
        ctx_1024 = 7.22013e-05 + 1.00017 * (_ctx_1024t + 0.3 * jax.random.normal(jax.random.fold_in(_rk, 611), (8, 77, 128), jnp.float32))
        return (x, ctx_1024)
    x, ctx_1024 = _rec_inputs()

    def _L0_attn_setup():
        import math
        import jax, jax.numpy as jnp
        import numpy as np
        B, C, D = (4, 256, 128)
        DQ = DV = 64
        H = 16
        key = jax.random.key(seed)
        kx, kq, kk, kv, kw = jax.random.split(key, 5)
        x = jax.random.normal(kx, (B, C, D), dtype=jnp.float32)
        Q = jax.random.normal(kq, (DQ, D, H), dtype=jnp.float32) / math.sqrt(D)
        K = jax.random.normal(kk, (DQ, D, H), dtype=jnp.float32) / math.sqrt(D)
        V = jax.random.normal(kv, (DV, D, H), dtype=jnp.float32) / math.sqrt(D)
        W = jax.random.normal(kw, (D, DV, H), dtype=jnp.float32) / math.sqrt(DV)
        return {'x': x, 'Q': Q, 'K': K, 'V': V, 'W': W}
    _L0_attn_all = _L0_attn_setup()
    _L0_attn_in = {k: v for k, v in _L0_attn_all.items() if k in ('Q', 'K', 'V', 'W')}
    del _L0_attn_all

    def _L0_xattn_setup():
        import jax, jax.numpy as jnp
        import numpy as np
        D_MODEL = 128
        B, S = (4, 256)
        key = jax.random.key(seed)
        ks = jax.random.split(key, 10)
        s = 1.0 / np.sqrt(D_MODEL)
        return {'k': jax.random.normal(ks[0], (B, S, D_MODEL), jnp.float32), 'v': jax.random.normal(ks[1], (B, S, D_MODEL), jnp.float32), 'q': jax.random.normal(ks[2], (B, S, D_MODEL), jnp.float32), 'Wk': jax.random.normal(ks[3], (D_MODEL, D_MODEL), jnp.float32) * s, 'Wv': jax.random.normal(ks[4], (D_MODEL, D_MODEL), jnp.float32) * s, 'bv': jnp.zeros((D_MODEL,), jnp.float32), 'Wq': jax.random.normal(ks[5], (D_MODEL, D_MODEL), jnp.float32) * s, 'bq': jnp.zeros((D_MODEL,), jnp.float32), 'Wo': jax.random.normal(ks[6], (D_MODEL, D_MODEL), jnp.float32) * s, 'bo': jnp.zeros((D_MODEL,), jnp.float32)}
    _L0_xattn_all = _L0_xattn_setup()
    _L0_xattn_in = {k: v for k, v in _L0_xattn_all.items() if k in ('Wk', 'Wv', 'bv', 'Wq', 'bq', 'Wo', 'bo')}
    del _L0_xattn_all

    def _L0_ffn_setup():
        import jax, jax.numpy as jnp
        import numpy as np
        TOP_K = 2
        CAPACITY_FACTOR = 1.25

        def _moe_forward(x, gate_w, wi_gate, wi_up, wo):
            B, S, D = x.shape
            E = wi_gate.shape[0]
            N = B * S
            capacity = max(int(N / E * CAPACITY_FACTOR), 1)
            x_flat = x.reshape(N, D)
            router_logits = x_flat @ gate_w.T
            router_probs = jax.nn.softmax(router_logits, axis=-1)
            top_k_probs, top_k_idx = jax.lax.top_k(router_probs, TOP_K)
            top_k_probs = top_k_probs / jnp.sum(top_k_probs, axis=-1, keepdims=True)
            out = jnp.zeros_like(x_flat)
            experts = jnp.arange(E, dtype=jnp.int32)
            for k in range(TOP_K):
                eid = top_k_idx[:, k]
                ew = top_k_probs[:, k]
                onehot = (eid[:, None] == experts[None, :]).astype(jnp.int32)
                pos_all = jnp.cumsum(onehot, axis=0) - 1
                pos = jnp.take_along_axis(pos_all, eid[:, None].astype(jnp.int32), axis=1)[:, 0]
                valid = pos < capacity
                pos_c = jnp.where(valid, pos, 0)
                disp = jnp.zeros((E, capacity, D), x_flat.dtype).at[eid, pos_c].add(jnp.where(valid[:, None], x_flat, 0.0))
                gate = jax.nn.silu(jnp.einsum('ecd,efd->ecf', disp, wi_gate))
                up = jnp.einsum('ecd,efd->ecf', disp, wi_up)
                expert_out = jnp.einsum('ecf,edf->ecd', gate * up, wo)
                tok_out = expert_out[eid, pos_c]
                out = out + jnp.where(valid[:, None], ew[:, None] * tok_out, 0.0)
            return out.reshape(B, S, D)
        key = jax.random.key(seed)
        k1, k2, k3, k4, k5 = jax.random.split(key, 5)
        B, S, D, F, E = (4, 256, 128, 512, 8)
        return {'x': jax.random.normal(k1, (B, S, D), dtype=jnp.float32), 'gate_w': jax.random.normal(k2, (E, D), dtype=jnp.float32) * 0.02, 'wi_gate': jax.random.normal(k3, (E, F, D), dtype=jnp.float32) * 0.02, 'wi_up': jax.random.normal(k4, (E, F, D), dtype=jnp.float32) * 0.02, 'wo': jax.random.normal(k5, (E, D, F), dtype=jnp.float32) * 0.02}
    _L0_ffn_all = _L0_ffn_setup()
    _L0_ffn_in = {k: v for k, v in _L0_ffn_all.items() if k in ('gate_w', 'wi_gate', 'wi_up', 'wo')}
    del _L0_ffn_all
    return {'x': x, 'ctx_1024': ctx_1024, 'L0_attn_Q': _L0_attn_in['Q'], 'L0_attn_K': _L0_attn_in['K'], 'L0_attn_V': _L0_attn_in['V'], 'L0_attn_W': _L0_attn_in['W'], 'L0_xattn_Wk': _L0_xattn_in['Wk'], 'L0_xattn_Wv': _L0_xattn_in['Wv'], 'L0_xattn_bv': _L0_xattn_in['bv'], 'L0_xattn_Wq': _L0_xattn_in['Wq'], 'L0_xattn_bq': _L0_xattn_in['bq'], 'L0_xattn_Wo': _L0_xattn_in['Wo'], 'L0_xattn_bo': _L0_xattn_in['bo'], 'L0_ffn_gate_w': _L0_ffn_in['gate_w'], 'L0_ffn_wi_gate': _L0_ffn_in['wi_gate'], 'L0_ffn_wi_up': _L0_ffn_in['wi_up'], 'L0_ffn_wo': _L0_ffn_in['wo']}

def reference(x, ctx_1024, L0_attn_Q, L0_attn_K, L0_attn_V, L0_attn_W, L0_xattn_Wk, L0_xattn_Wv, L0_xattn_bv, L0_xattn_Wq, L0_xattn_bq, L0_xattn_Wo, L0_xattn_bo, L0_ffn_gate_w, L0_ffn_wi_gate, L0_ffn_wi_up, L0_ffn_wo):
    import jax
    import jax.numpy as jnp

    def _L0_attn_ref(x, Q, K, V, W):
        import math
        import jax, jax.numpy as jnp
        import numpy as np
        B, C, D = (4, 256, 128)
        DQ = DV = 64
        H = 16
        d_query, d_embed, num_heads = Q.shape
        d_value = V.shape[0]
        sq = math.sqrt(d_query / d_embed)
        sv = math.sqrt(d_value / d_embed)
        q = jnp.einsum('qdh,bcd->bhcq', Q, x) * sq
        k = jnp.einsum('qdh,bcd->bhcq', K, x) * sq
        v = jnp.einsum('vdh,bcd->bhcv', V, x) * sv
        att = jnp.einsum('bhcq,bhCq->bhcC', q, k) / d_query
        T = x.shape[1]
        causal = jnp.arange(T)[:, None] >= jnp.arange(T)[None, :]
        att = jnp.where(causal, att, -jnp.inf)
        p = jax.nn.softmax(att, axis=-1)
        y = jnp.einsum('bhcC,bhCv->bhcv', p, v)
        z = jnp.einsum('dvh,bhcv->bcd', W, y) * (math.sqrt(d_embed / d_value) / num_heads)
        return z

    def _L0_xattn_ref(k, v, q, Wk, Wv, bv, Wq, bq, Wo, bo):
        import jax, jax.numpy as jnp
        import numpy as np
        D_MODEL = 128
        B, S = (4, 256)
        kp = jnp.einsum('bsd,ed->bse', k, Wk)
        vp = jnp.einsum('bsd,ed->bse', v, Wv) + bv
        qp = jnp.einsum('bsd,ed->bse', q, Wq) + bq
        scale = 1.0 / jnp.sqrt(jnp.float32(kp.shape[-1]))
        scores = jnp.einsum('bqd,bkd->bqk', qp, kp) * scale
        probs = jax.nn.softmax(scores, axis=-1)
        ctx = jnp.einsum('bqk,bkd->bqd', probs, vp)
        return jnp.einsum('bqd,ed->bqe', ctx, Wo) + bo

    def _L0_ffn_ref(x, gate_w, wi_gate, wi_up, wo):
        import jax, jax.numpy as jnp
        import numpy as np
        TOP_K = 2
        CAPACITY_FACTOR = 1.25

        def _moe_forward(x, gate_w, wi_gate, wi_up, wo):
            B, S, D = x.shape
            E = wi_gate.shape[0]
            N = B * S
            capacity = max(int(N / E * CAPACITY_FACTOR), 1)
            x_flat = x.reshape(N, D)
            router_logits = x_flat @ gate_w.T
            router_probs = jax.nn.softmax(router_logits, axis=-1)
            top_k_probs, top_k_idx = jax.lax.top_k(router_probs, TOP_K)
            top_k_probs = top_k_probs / jnp.sum(top_k_probs, axis=-1, keepdims=True)
            out = jnp.zeros_like(x_flat)
            experts = jnp.arange(E, dtype=jnp.int32)
            for k in range(TOP_K):
                eid = top_k_idx[:, k]
                ew = top_k_probs[:, k]
                onehot = (eid[:, None] == experts[None, :]).astype(jnp.int32)
                pos_all = jnp.cumsum(onehot, axis=0) - 1
                pos = jnp.take_along_axis(pos_all, eid[:, None].astype(jnp.int32), axis=1)[:, 0]
                valid = pos < capacity
                pos_c = jnp.where(valid, pos, 0)
                disp = jnp.zeros((E, capacity, D), x_flat.dtype).at[eid, pos_c].add(jnp.where(valid[:, None], x_flat, 0.0))
                gate = jax.nn.silu(jnp.einsum('ecd,efd->ecf', disp, wi_gate))
                up = jnp.einsum('ecd,efd->ecf', disp, wi_up)
                expert_out = jnp.einsum('ecf,edf->ecd', gate * up, wo)
                tok_out = expert_out[eid, pos_c]
                out = out + jnp.where(valid[:, None], ew[:, None] * tok_out, 0.0)
            return out.reshape(B, S, D)
        return _moe_forward(x, gate_w, wi_gate, wi_up, wo)
    x = x + _L0_attn_ref(_layernorm(x, axis=-1), L0_attn_Q, L0_attn_K, L0_attn_V, L0_attn_W)
    x = x + _L0_xattn_ref(ctx_1024, ctx_1024, _layernorm(x, axis=-1), L0_xattn_Wk, L0_xattn_Wv, L0_xattn_bv, L0_xattn_Wq, L0_xattn_bq, L0_xattn_Wo, L0_xattn_bo)
    x = x + _L0_ffn_ref(_layernorm(x, axis=-1), L0_ffn_gate_w, L0_ffn_wi_gate, L0_ffn_wi_up, L0_ffn_wo)
    return x

_drawn_inputs = setup_inputs


def setup_inputs(seed=0):
    import zlib

    import numpy as np

    out = dict(_drawn_inputs(seed))
    spreads = {'L0_xattn_bv': (0.0, 0.1), 'L0_xattn_bq': (0.0, 0.332), 'L0_xattn_bo': (0.0, 0.1)}
    factors = {'L0_attn_Q': 8.0,
     'L0_attn_K': 8.0,
     'L0_ffn_gate_w': 8.0,
     'L0_ffn_wi_gate': 8.0,
     'L0_ffn_wi_up': 8.0,
     'L0_ffn_wo': 8.0}
    for name, (base, spread) in spreads.items():
        noise = np.random.default_rng([zlib.crc32(name.encode()), seed]).standard_normal(out[name].shape)
        drawn = base * np.exp(spread * noise) if base else spread * noise
        out[name] = jnp.asarray(drawn.astype(out[name].dtype))
    for name, factor in factors.items():
        out[name] = (out[name] * factor).astype(out[name].dtype)
    return out
```

```python
from contextlib import ExitStack

import concourse.bass as bass
from concourse import mybir

F32 = mybir.dt.float32
BF16 = mybir.dt.bfloat16
I32 = mybir.dt.int32
U32 = mybir.dt.uint32
ALU = mybir.AluOpType
ACT = mybir.ActivationFunctionType
AX_X = mybir.AxisListType.X


def decoder_layer(nc, x, ctxT, q_w, k_w, v_w, w_w, wkT, wvT, bv, wq, bq, woT, bo, gate_wT,
                  wgT, wuT, wdT, out):
    B, T, D = x.shape
    H = 2 * q_w.shape[1]
    DQ = q_w.shape[0] // 2
    DV = v_w.shape[1] // H
    S2 = ctxT.shape[1] // B
    E, F = wgT.shape[1:]
    N = B * T
    CAP = max(int(N / E * 1.25), 1)
    SLOTS = 2 * CAP
    P = 128
    assert T == P and D == P and 2 * DV == P and 2 * DQ == P
    GH = 4
    NG = H // GH
    G = B * NG
    NP = H // 2
    FC = F // P
    TILES = [(t, min(P, SLOTS - t)) for t in range(0, SLOTS, P)]
    NT = len(TILES)
    ROW = D + 2
    EPS = 1e-5
    BIG = 1e30
    A_SCALE = -(DQ / D) / DQ
    Z_SCALE = (DV / D) ** 0.5 * (D / DV) ** 0.5 / H
    X_SCALE = -float(D) ** -0.5
    HALF = B * S2 // 2

    disp = nc.dram_tensor("dispatched_rows", [E * SLOTS + 2 * P, ROW], F32).ap()
    acc = nc.dram_tensor("accumulated_out", [N + P, D], F32).ap()

    with ExitStack() as ctx:
        def sb(name, shape, dt=F32):
            return ctx.enter_context(nc.sbuf_tensor(name, shape, dt))

        def sem(name):
            return ctx.enter_context(nc.semaphore(name))

        x_sb = sb("x_sb", [P, B, D])
        x1 = sb("x1", [P, 2, D])
        x2 = sb("x2", [P, B, D])
        ctxT_sb = sb("ctxT_sb", [P, B * S2])
        qw_sb = sb("qw_sb", [P, H // 2, D])
        kw_sb = sb("kw_sb", [P, H // 2, D])
        vw_sb = sb("vw_sb", [P, H * DV])
        ww_sb = sb("ww_sb", [P, NP, D])
        wkT_sb = sb("wkT_sb", [P, D])
        wvT_sb = sb("wvT_sb", [P, D])
        wq_sb = sb("wq_sb", [P, D])
        woT_sb = sb("woT_sb", [P, D])
        bv_sb = sb("bv_sb", [P, 1])
        bq_sb = sb("bq_sb", [P, 1])
        bo_bc = sb("bo_bc", [S2, D])
        gw_sb = sb("gw_sb", [P, E])
        wg_sb = sb("wg_sb", [P, E, F])
        wu_sb = sb("wu_sb", [P, E, F])
        wd_sb = sb("wd_sb", [P, E, FC, D])

        ident = sb("ident", [P, P])
        ident_b = sb("ident_b", [P, P], BF16)
        causal = sb("causal", [P, GH, P], BF16)
        before = sb("before", [P, P], BF16)
        ones_b = sb("ones_b", [P, P], BF16)
        iota_e = sb("iota_e", [P, 2, E])
        choice_base = sb("choice_base", [P, 2])
        dump_row = sb("dump_row", [P, 2])
        minus_half = sb("minus_half", [P, B])
        blank = sb("blank", [P, E, ROW])

        xn = sb("xn", [P, B, D])
        xnT = sb("xnT", [P, B, T])
        stat1 = sb("stat1", [P, B, 6])
        mv1 = sb("mv1", [P, B, 2])
        ve1 = sb("ve1", [P, B])
        rstd1 = sb("rstd1", [P, B])
        A_sb = sb("A_sb", [P, H, D])
        tT_sb = sb("tT_sb", [P, 4, GH, T])
        v_sb = sb("v_sb", [P, 2, H, DV])
        smin = sb("smin", [P, 4, GH])
        ssum = sb("ssum", [P, 4, GH])
        sinv = sb("sinv", [P, 4, GH])
        p_sb = sb("p_sb", [P, 3, GH, T])
        pn_sb = sb("pn_sb", [P, 3, GH, T])
        pT_sb = sb("pT_sb", [P, 3, GH, T])
        yT_sb = sb("yT_sb", [P, 2, NP, T])

        kpT = sb("kpT", [P, B * S2])
        vpT = sb("vpT", [P, B * S2])
        qk2 = sb("qk2", [P, B * S2])
        qbias = sb("qbias", [P, B * S2])
        bq_bc = sb("bq_bc", [P, P])
        vo = sb("vo", [S2, B, D])
        stat = sb("stat", [P, 2, 6])
        mv = sb("mv", [P, 2, 2])
        ve = sb("ve", [P, 2])
        rstd = sb("rstd", [P, 2])
        xn2 = sb("xn2", [P, D])
        xn2T = sb("xn2T", [P, T])
        s2_sb = sb("s2_sb", [P, S2])
        s2min = sb("s2min", [P, 1])
        p2 = sb("p2", [P, S2])
        s2sum = sb("s2sum", [P, 1])
        s2inv = sb("s2inv", [P, 1])
        p2T = sb("p2T", [S2, T])
        rows = sb("rows", [P, B, 2, ROW])
        xn3T = sb("xn3T", [P, T])
        logit = sb("logit", [P, E])
        top8 = sb("top8", [P, 8])
        idx8 = sb("idx8", [P, 8], U32)
        idxf = sb("idxf", [P, 2])
        ratio = sb("ratio", [P, 1])
        denom = sb("denom", [P, 1])
        wts = sb("wts", [P, 2])
        oh = sb("oh", [P, 2, E], BF16)
        taken = sb("taken", [P, 2, E], BF16)
        sbase = sb("sbase", [P, 2])
        prod = sb("prod", [P, 2, E])
        pos = sb("pos", [P, 2])
        rel = sb("rel", [P, 2])
        relok = sb("relok", [P, 2])
        slot = sb("slot", [P, B, 2], I32)

        dsp = sb("dsp", [P, E, NT, ROW])
        dT = sb("dT", [P, 2, SLOTS])
        sg = sb("sg", [P, 2, SLOTS])
        hT = sb("hT", [P, 2, FC, SLOTS])
        eo = sb("eo", [P, 2, NT, D])

        ps = ctx.enter_context(nc.psum_tensor("ps", [P, 8, 512], F32))
        PROJ, SC, PT, YB, MB = [0, 1], [2, 3], [4, 5], 6, 7
        GATE, UP, OUT_B, DT = [0, 1], [2, 3], [4, 5], [6, 7]

        names = """x_in qk_in vw_in ctx_in small_in gate_in consts_ok blank_ok blank_out
        stat1_ok mv1_ok rstd1_ok xn_ok xnT_ps xnT_ok A_ps A_ok
        t_ps t_ok v_ps v_ok s_ps min_ok exp_ok sinv_ok pn_ok pt_ps pt_ok y_ps y_ok
        pre_ps pre_ok vo_ps vo_ok z_ps x1_ok stat_ok mv_ok ve_ok rstd_ok xn2_ok xn2T_ps xn2T_ok s2_ps
        s2min_ok p2_ok p2T_ps p2T_ok o2_ps x2_ok xn3_ok xn3T_ps xn3T_ok lg_ps lg_ok top_ok ratio_ok
        wts_ok oh_ok pf_ps taken_ok slot_ok acc_out dve_step pool_step scattered
        dT_ps dT_ok g_ps u_ps sg_ok h_ok o_ps eo_ok added final""".split()
        S = {n: sem(n) for n in names}
        ffn_in = [sem(f"ffn_in{e}") for e in range(E)]
        rows_in = [sem(f"rows_in{e}") for e in range(E)]

        CH = ["z", "tr2", "sc2", "trp2", "o2", "tr3", "lg", "pf"]
        STEPS = range(-2, G + 6)

        def chain_at(n, half):
            b, k = divmod(2 * (n - 5) + half, 2 * NG)
            return (b, CH[k]) if 0 <= b < B else None

        block = ctx.enter_context(nc.Block())

        @block.sync
        def _(sp):
            for h in range(2):
                sp.dma_start(x_sb[:, 4 * h:4 * h + 4, :], x[4 * h:4 * h + 4].rearrange("b t d -> t b d")) \
                    .then_inc(S["x_in"], 16)
                if h == 0:
                    sp.wait_ge(S["x_in"], 16)
            sp.dma_start(vw_sb[:, :], v_w).then_inc(S["vw_in"], 16)
            sp.dma_start(ww_sb[:, :, :], w_w).then_inc(S["vw_in"], 16)
            sp.dma_start(gw_sb[:, :], gate_wT).then_inc(S["gate_in"], 16)
            sp.wait_ge(S["blank_ok"], 4)
            for i, (t, m) in enumerate(TILES):
                dst = disp[0:E * SLOTS, :].rearrange("(e s) r -> s e r", e=E)
                sp.dma_start(dst[t:t + m], blank[0:m, :, :]).then_inc(S["blank_out"], 16)
            sp.dma_start(acc[N:N + P, :], blank[:, 0, 0:D]).then_inc(S["blank_out"], 16)
            for e in range(E):
                sp.dma_start(wg_sb[:, e, :], wgT[:, e, :]).then_inc(ffn_in[e], 16)
                sp.dma_start(wu_sb[:, e, :], wuT[:, e, :]).then_inc(ffn_in[e], 16)
                sp.dma_start(wd_sb[:, e, :, :], wdT[:, e, :, :]).then_inc(ffn_in[e], 16)
            for b in range(B):
                sp.wait_ge(S["x2_ok"], b + 1)
                sp.dma_start(acc[b * T:(b + 1) * T, :], x2[:, b, :]).then_inc(S["acc_out"], 16)
            sp.wait_ge(S["scattered"], 2 * B * 16)
            for e in range(E):
                for i, (t, m) in enumerate(TILES):
                    r = e * SLOTS + t
                    sp.dma_start(dsp[0:m, e, i, :], disp[r:r + m, :]).then_inc(rows_in[e], 16)
            sp.wait_ge(S["added"], 16 * NT * E)
            sp.dma_start(out.rearrange("b t d -> (b t) d"), acc[0:N, :]).then_inc(S["final"], 16)
            sp.wait_ge(S["final"], 16)

        @block.gpsimd
        def _(pool):
            g = nc.gpsimd
            n_link = [0]

            def link(ins):
                n_link[0] += 1
                ins.then_inc(S["pool_step"], 1)
                pool.wait_ge(S["pool_step"], n_link[0])

            g.memset(minus_half[:, :], -0.5)
            link(g.memset(ident[:, :], 0.0))
            link(g.affine_select(out=ident[:, :], in_=ident[:, :], compare_op=ALU.not_equal, fill=1.0,
                                 base=0, pattern=[[-1, P]], channel_multiplier=1))
            g.tensor_copy(ident_b[:, :], ident[:, :])
            link(g.memset(causal[:, :, :], 0.0))
            g.affine_select(out=causal[:, :, :], in_=causal[:, :, :], compare_op=ALU.is_ge, fill=BIG,
                            base=0, pattern=[[0, GH], [-1, P]], channel_multiplier=1)
            link(g.memset(before[:, :], 1.0))
            g.affine_select(out=before[:, :], in_=before[:, :], compare_op=ALU.is_ge, fill=0.0,
                            base=-1, pattern=[[1, P]], channel_multiplier=-1)
            g.memset(ones_b[:, :], 1.0)
            g.iota(iota_e[:, :, :], pattern=[[0, 2], [1, E]], base=0, channel_multiplier=0,
                   allow_small_or_imprecise_dtypes=True)
            g.iota(choice_base[:, :], pattern=[[CAP, 2]], base=0, channel_multiplier=0,
                   allow_small_or_imprecise_dtypes=True)
            g.iota(dump_row[:, :], pattern=[[P, 2]], base=E * SLOTS, channel_multiplier=1,
                   allow_small_or_imprecise_dtypes=True)
            g.memset(taken[:, :, :], 0.0)
            g.iota(rows[:, :, :, D + 1].bitcast(I32), pattern=[[T, B], [0, 2]], base=0,
                   channel_multiplier=1).then_inc(S["consts_ok"], 1)
            g.memset(blank[:, :, 0:D + 1], 0.0).then_inc(S["blank_ok"], 2)
            g.iota(blank[:, :, D + 1].bitcast(I32), pattern=[[0, E]], base=N,
                   channel_multiplier=1).then_inc(S["blank_ok"], 2)

            pool.wait_ge(S["mv1_ok"], 1)
            link(g.tensor_scalar(ve1[:, :], mv1[:, :, 1], EPS, None, ALU.add))
            g.tensor_tensor(rstd1[:, :], ve1[:, :], minus_half[:, :], ALU.pow).then_inc(S["rstd1_ok"], 1)

            def rstd_of(k, count):
                pool.wait_ge(S["mv_ok"], count)
                g.tensor_scalar(ve[:, k:k + 1], mv[:, k, 1:2], EPS, None, ALU.add).then_inc(S["ve_ok"], 1)
                pool.wait_ge(S["ve_ok"], count)
                g.tensor_tensor(rstd[:, k:k + 1], ve[:, k:k + 1], minus_half[:, 0:1], ALU.pow) \
                    .then_inc(S["rstd_ok"], 1)

            def chain(n, half):
                at = chain_at(n, half)
                if at is None:
                    return
                b, k = at
                if k == "z":
                    rstd_of(0, 2 * b + 1)
                elif k == "o2":
                    rstd_of(1, 2 * b + 2)
                elif k == "pf":
                    if b == 0:
                        pool.wait_ge(S["blank_out"], 16 * (NT + 1))
                    pool.wait_ge(S["slot_ok"], b + 1)
                    for c in range(2):
                        if b or c:
                            pool.wait_ge(S["scattered"], 16 * (2 * b + c))
                        pool.indirect_dma_start(
                            out=disp, out_offset=bass.IndirectOffsetOnAxis(ap=slot[:, b, c:c + 1], axis=0),
                            in_=rows[:, b, c, :], in_offset=None).then_inc(S["scattered"], 16)

            for n in STEPS:
                if 0 <= n < G:
                    pool.wait_ge(S["sinv_ok"], n + 1)
                    if n >= 3:
                        pool.wait_ge(S["pt_ps"], n - 2)
                    g.tensor_tensor(pn_sb[:, n % 3, :, :], p_sb[:, n % 3, :, :],
                                    sinv[:, n % 4, :].unsqueeze(2).to_broadcast([P, GH, T]), ALU.mult) \
                        .then_inc(S["pn_ok"], 1)
                chain(n, 0)
                chain(n, 1)

            pool.wait_ge(S["acc_out"], 16 * B)
            for e in range(E):
                pool.wait_ge(S["eo_ok"], NT * (e + 1))
                if e:
                    pool.wait_ge(S["added"], 16 * NT * e)
                for i, (t, m) in enumerate(TILES):
                    if i:
                        pool.wait_ge(S["added"], 16 * (NT * e + i))
                    pool.indirect_dma_start(
                        out=acc, out_offset=bass.IndirectOffsetOnAxis(
                            ap=dsp[0:m, e, i, D + 1:D + 2].bitcast(I32), axis=0),
                        in_=eo[0:m, e % 2, i, :], in_offset=None, compute_op=ALU.add) \
                        .then_inc(S["added"], 16)

        @block.scalar
        def _(act):
            a = nc.scalar
            act.dma_start(qw_sb[:, :, :], q_w).then_inc(S["qk_in"], 16)
            act.dma_start(kw_sb[:, :, :], k_w).then_inc(S["qk_in"], 16)
            act.dma_start(ctxT_sb[:, :], ctxT).then_inc(S["ctx_in"], 16)
            for dst, src in ((wkT_sb, wkT), (wvT_sb, wvT), (wq_sb, wq), (woT_sb, woT),
                             (bv_sb, bv.rearrange("(p a) -> p a", a=1)),
                             (bq_sb, bq.rearrange("(p a) -> p a", a=1)),
                             (bo_bc, bo.rearrange("(a d) -> a d", a=1).to_broadcast([S2, D]))):
                act.dma_start(dst[:, :], src).then_inc(S["small_in"], 16)

            for i in range(NG):
                act.wait_ge(S["A_ps"], i + 1)
                a.activation(A_sb[:, GH * i:GH * i + GH, :], ps[:, SC[i % 2], :], ACT.Copy,
                             scale=A_SCALE).then_inc(S["A_ok"], 1)

            def copy_t(n):
                act.wait_ge(S["t_ps"], n + 1)
                if n >= 4:
                    act.wait_ge(S["s_ps"], n - 3)
                a.copy(tT_sb[:, n % 4, :, :], ps[:, PROJ[n % 2], :]).then_inc(S["t_ok"], 1)

            def exps(n):
                act.wait_ge(S["min_ok"], n + 1)
                if n >= 3:
                    act.wait_ge(S["pn_ok"], n - 2)
                if n >= 4:
                    act.wait_ge(S["sinv_ok"], n - 3)
                for h in range(GH):
                    last = a.activation(p_sb[:, n % 3, h, :], ps[:, SC[n % 2], h * T:(h + 1) * T], ACT.Exp,
                                        bias=smin[:, n % 4, h:h + 1], scale=-1.0,
                                        accum_out=ssum[:, n % 4, h:h + 1])
                last.then_inc(S["exp_ok"], 1)

            def chain(n, half):
                at = chain_at(n, half)
                if at is None:
                    return
                b, k = at
                if k == "tr2":
                    act.wait_ge(S["xn2T_ps"], b + 1)
                    a.copy(xn2T[:, :], ps[:, MB, 0:T]).then_inc(S["xn2T_ok"], 1)
                elif k == "sc2":
                    act.wait_ge(S["s2min_ok"], b + 1)
                    a.activation(p2[:, :], s2_sb[:, :], ACT.Exp, bias=s2min[:, :], scale=-1.0,
                                 accum_out=s2sum[:, :]).then_inc(S["p2_ok"], 1)
                elif k == "trp2":
                    act.wait_ge(S["p2T_ps"], b + 1)
                    a.copy(p2T[:, :], ps[0:S2, MB, 0:T]).then_inc(S["p2T_ok"], 1)
                elif k == "tr3":
                    act.wait_ge(S["xn3T_ps"], b + 1)
                    a.copy(xn3T[:, :], ps[:, MB, 0:T]).then_inc(S["xn3T_ok"], 1)
                elif k == "lg":
                    act.wait_ge(S["lg_ps"], b + 1)
                    if b:
                        act.wait_ge(S["oh_ok"], b)
                    a.copy(logit[:, :], ps[:, MB, 0:E]).then_inc(S["lg_ok"], 1)
                    act.wait_ge(S["top_ok"], b + 1)
                    a.activation(ratio[:, :], top8[:, 0:1], ACT.Exp, bias=top8[:, 1:2], scale=-1.0) \
                        .then_inc(S["ratio_ok"], 1)

            for n in STEPS:
                if n + 2 < G:
                    copy_t(n + 2)
                if 0 <= n + 1 < G:
                    exps(n + 1)
                chain(n, 0)
                chain(n, 1)

            def weigh(e):
                act.wait_ge(S["o_ps"], e + 1)
                if e >= 2:
                    act.wait_ge(S["added"], 16 * NT * (e - 1))
                for i, (t, m) in enumerate(TILES):
                    a.activation(eo[0:m, e % 2, i, :], ps[0:m, OUT_B[e % 2], i * D:(i + 1) * D], ACT.Copy,
                                         scale=dsp[0:m, e, i, D:D + 1]).then_inc(S["eo_ok"], 1)

            for e in range(E):
                for f in range(FC):
                    i = e * FC + f
                    act.wait_ge(S["g_ps"], i + 1)
                    if i >= 2:
                        act.wait_ge(S["h_ok"], i - 1)
                    a.activation(sg[:, i % 2, :], ps[:, GATE[i % 2], 0:SLOTS], ACT.Silu) \
                        .then_inc(S["sg_ok"], 1)
                if e:
                    weigh(e - 1)
            weigh(E - 1)

        @block.vector
        def _(dve):
            v = nc.vector
            n_link = [0]

            def link(ins):
                n_link[0] += 1
                ins.then_inc(S["dve_step"], 1)
                dve.wait_ge(S["dve_step"], n_link[0])

            for b in range(B):
                if b % 4 == 0:
                    dve.wait_ge(S["x_in"], 16 * (b // 4 + 1))
                v.bn_stats(stat1[:, b, :], x_sb[:, b, :]).then_inc(S["stat1_ok"], 1)
            dve.wait_ge(S["stat1_ok"], B)
            for b in range(B):
                last = v.bn_aggr(mv1[:, b, :], stat1[:, b, :])
            last.then_inc(S["mv1_ok"], 1)
            dve.wait_ge(S["rstd1_ok"], 1)
            dve.wait_ge(S["mv1_ok"], 1)
            for b in range(B):
                v.tensor_scalar(xn[:, b, :], x_sb[:, b, :], mv1[:, b, 0:1], rstd1[:, b:b + 1],
                                ALU.subtract, ALU.mult).then_inc(S["xn_ok"], 1)
            for i in range(B // 4):
                dve.wait_ge(S["xnT_ps"], i + 1)
                v.tensor_copy(xnT[:, 4 * i:4 * i + 4, :], ps[:, PT[i], :]).then_inc(S["xnT_ok"], 1)

            def copy_v(b):
                for i in range(2):
                    dve.wait_ge(S["v_ps"], 2 * b + i + 1)
                    if b >= 2:
                        dve.wait_ge(S["y_ps"], NG * (b - 1))
                    v.tensor_copy(v_sb[:, b % 2, i * (H // 2):(i + 1) * (H // 2), :], ps[:, PROJ[i], :]) \
                        .then_inc(S["v_ok"], 1)

            def row_min(n):
                dve.wait_ge(S["s_ps"], n + 1)
                if n >= 4:
                    dve.wait_ge(S["exp_ok"], n - 3)
                v.tensor_reduce(smin[:, n % 4, :], ps[:, SC[n % 2], :].rearrange("p (h c) -> p h c", h=GH),
                                axis=AX_X, op=ALU.min).then_inc(S["min_ok"], 1)

            def inverse(n):
                dve.wait_ge(S["exp_ok"], n + 1)
                if n >= 4:
                    dve.wait_ge(S["pn_ok"], n - 3)
                v.reciprocal(sinv[:, n % 4, :], ssum[:, n % 4, :]).then_inc(S["sinv_ok"], 1)

            def copy_pt(n):
                dve.wait_ge(S["pt_ps"], n + 1)
                if n >= 3:
                    dve.wait_ge(S["y_ps"], n - 2)
                v.tensor_copy(pT_sb[:, n % 3, :, :], ps[:, PT[n % 2], :]).then_inc(S["pt_ok"], 1)

            def copy_y(i):
                dve.wait_ge(S["y_ps"], 2 * i + 2)
                b, k = divmod(i, 2)
                if b >= 2:
                    dve.wait_ge(S["z_ps"], b - 1)
                v.tensor_copy(yT_sb[:, b % 2, 4 * k:4 * k + 4, :], ps[:, YB, :]).then_inc(S["y_ok"], 1)

            def pre_copy(i):
                dve.wait_ge(S["pre_ps"], i + 1)
                k, h = divmod(i, 2)
                cols = slice(h * HALF, (h + 1) * HALF)
                src = ps[:, MB, 0:HALF]
                if k == 0:
                    ins = v.tensor_scalar(kpT[:, cols], src, X_SCALE, None, ALU.mult)
                elif k == 1:
                    ins = v.tensor_scalar(vpT[:, cols], src, bv_sb[:, 0:1], None, ALU.add)
                elif k == 2:
                    ins = v.tensor_copy(qk2[:, cols], src)
                else:
                    ins = v.tensor_copy(qbias[:, cols], src)
                ins.then_inc(S["pre_ok"], 1)

            def pre_vo(i):
                dve.wait_ge(S["vo_ps"], i + 1)
                v.tensor_tensor(vo[:, 4 * i:4 * i + 4, :], ps[0:S2, MB, :].rearrange("p (b d) -> p b d", b=4),
                                bo_bc[:, :].unsqueeze(1).to_broadcast([S2, 4, D]), ALU.add) \
                    .then_inc(S["vo_ok"], 1)

            def stats(k, src):
                link(v.bn_stats(stat[:, k, :], src))
                v.bn_aggr(mv[:, k, :], stat[:, k, :]).then_inc(S["mv_ok"], 1)

            def chain(n, half):
                at = chain_at(n, half)
                if at is None:
                    return
                b, k = at
                if k == "z":
                    dve.wait_ge(S["z_ps"], b + 1)
                    v.scalar_tensor_tensor(out=x1[:, b % 2, :], in0=ps[:, MB, 0:D], scalar=Z_SCALE,
                                           in1=x_sb[:, b, :], op0=ALU.mult, op1=ALU.add) \
                        .then_inc(S["x1_ok"], 1)
                    dve.wait_ge(S["x1_ok"], b + 1)
                    stats(0, x1[:, b % 2, :])
                    dve.wait_ge(S["rstd_ok"], 2 * b + 1)
                    v.tensor_scalar(xn2[:, :], x1[:, b % 2, :], mv[:, 0, 0:1], rstd[:, 0:1],
                                    ALU.subtract, ALU.mult).then_inc(S["xn2_ok"], 1)
                elif k == "sc2":
                    dve.wait_ge(S["s2_ps"], b + 1)
                    if b:
                        dve.wait_ge(S["p2_ok"], b)
                    v.tensor_tensor_reduce(out=s2_sb[:, :], in0=ps[:, MB, 0:S2],
                                           in1=qbias[:, b * S2:(b + 1) * S2], scale=1.0, scalar=3e38,
                                           op0=ALU.add, op1=ALU.min, accum_out=s2min[:, :]) \
                        .then_inc(S["s2min_ok"], 1)
                elif k == "trp2":
                    dve.wait_ge(S["p2_ok"], b + 1)
                    v.reciprocal(s2inv[:, :], s2sum[:, :]).then_inc(S["dve_step"], 1)
                    n_link[0] += 1
                elif k == "o2":
                    dve.wait_ge(S["o2_ps"], b + 1)
                    dve.wait_ge(S["dve_step"], n_link[0])
                    v.scalar_tensor_tensor(out=x2[:, b, :], in0=ps[:, MB, 0:D], scalar=s2inv[:, 0:1],
                                           in1=x1[:, b % 2, :], op0=ALU.mult, op1=ALU.add) \
                        .then_inc(S["x2_ok"], 1)
                    dve.wait_ge(S["x2_ok"], b + 1)
                    stats(1, x2[:, b, :])
                    dve.wait_ge(S["rstd_ok"], 2 * b + 2)
                    v.tensor_scalar(rows[:, b, :, 0:D], x2[:, b, :].unsqueeze(1).to_broadcast([P, 2, D]),
                                    mv[:, 1, 0:1], rstd[:, 1:2], ALU.subtract, ALU.mult) \
                        .then_inc(S["xn3_ok"], 1)
                elif k == "lg":
                    dve.wait_ge(S["lg_ok"], b + 1)
                    if b:
                        dve.wait_ge(S["ratio_ok"], b)
                    v.max(top8[:, :], logit[:, :]).then_inc(S["top_ok"], 1)
                    dve.wait_ge(S["top_ok"], b + 1)
                    link(v.max_index(idx8[:, :], top8[:, :], logit[:, :]))
                    link(v.tensor_copy(idxf[:, :], idx8[:, 0:2]))
                    v.tensor_tensor(oh[:, :, :], iota_e[:, :, :], idxf[:, :].unsqueeze(2).to_broadcast([P, 2, E]),
                                    ALU.is_equal).then_inc(S["oh_ok"], 1)
                    link(v.scalar_tensor_tensor(out=sbase[:, :], in0=idxf[:, :], scalar=float(SLOTS),
                                                in1=choice_base[:, :], op0=ALU.mult, op1=ALU.add))
                    link(v.tensor_tensor(sbase[:, :], sbase[:, :], dump_row[:, :], ALU.subtract))
                    dve.wait_ge(S["ratio_ok"], b + 1)
                    link(v.tensor_scalar(denom[:, :], ratio[:, :], 1.0, None, ALU.add))
                    link(v.reciprocal(wts[:, 0:1], denom[:, :]))
                    link(v.tensor_tensor(wts[:, 1:2], ratio[:, :], wts[:, 0:1], ALU.mult))
                    v.tensor_copy(rows[:, b, :, D], wts[:, :]).then_inc(S["wts_ok"], 1)
                elif k == "pf":
                    dve.wait_ge(S["pf_ps"], b + 1)
                    dve.wait_ge(S["oh_ok"], b + 1)
                    link(v.tensor_tensor(prod[:, :, :], ps[:, MB, 0:2 * E].rearrange("p (k e) -> p k e", k=2),
                                         oh[:, :, :], ALU.mult))
                    v.tensor_tensor(taken[:, :, :], taken[:, :, :], oh[:, :, :], ALU.add) \
                        .then_inc(S["taken_ok"], 1)
                    link(v.tensor_reduce(pos[:, :], prod[:, :, :], axis=AX_X, op=ALU.add))
                    link(v.tensor_tensor(rel[:, :], pos[:, :], sbase[:, :], ALU.add))
                    link(v.scalar_tensor_tensor(out=relok[:, :], in0=pos[:, :], scalar=float(CAP),
                                                in1=rel[:, :], op0=ALU.is_lt, op1=ALU.mult))
                    dve.wait_ge(S["wts_ok"], b + 1)
                    v.tensor_tensor(slot[:, b, :], relok[:, :], dump_row[:, :], ALU.add) \
                        .then_inc(S["slot_ok"], 1)

            dve.wait_ge(S["consts_ok"], 1)
            for n in STEPS:
                if n == -2:
                    dve.wait_ge(S["ctx_in"], 16)
                    dve.wait_ge(S["small_in"], 16 * 7)
                    v.tensor_copy(bq_bc[:, :], bq_sb[:, 0:1].to_broadcast([P, P])).then_inc(S["pre_ok"], 1)
                if n + 2 < G and (n + 2) % NG == 1:
                    copy_v((n + 2) // NG)
                if 0 <= n + 1 < G:
                    row_min(n + 1)
                chain(n, 0)
                if 0 <= n < G:
                    copy_pt(n)
                chain(n, 1)
                if 1 <= n <= G and n % 2 == 0:
                    copy_y(n // 2 - 1)
                if n == 1:
                    for i in range(8):
                        pre_copy(i)
                    for i in range(2):
                        pre_vo(i)
                if 0 <= n + 1 < G:
                    inverse(n + 1)

            def copy_dt(e):
                dve.wait_ge(S["dT_ps"], e + 1)
                if e >= 2:
                    dve.wait_ge(S["u_ps"], FC * (e - 1))
                v.tensor_copy(dT[:, e % 2, :], ps[:, DT[e % 2], 0:SLOTS]).then_inc(S["dT_ok"], 1)

            copy_dt(0)
            for e in range(E):
                for f in range(FC):
                    i = e * FC + f
                    dve.wait_ge(S["sg_ok"], i + 1)
                    dve.wait_ge(S["u_ps"], i + 1)
                    if e >= 2 and f == 0:
                        dve.wait_ge(S["o_ps"], e - 1)
                    v.tensor_tensor(hT[:, e % 2, f, :], ps[:, UP[i % 2], 0:SLOTS], sg[:, i % 2, :], ALU.mult) \
                        .then_inc(S["h_ok"], 1)
                    if f == 1 and e + 1 < E:
                        copy_dt(e + 1)

        @block.tensor
        def _(pe):
            mm = nc.tensor.matmul
            pe.wait_ge(S["qk_in"], 32)
            for i in range(NG):
                if i >= 2:
                    pe.wait_ge(S["A_ok"], i - 1)
                for j in range(GH):
                    r, k = divmod(GH * i + j, H // 2)
                    last = mm(ps[:, SC[i % 2], j * D:(j + 1) * D], qw_sb[r * DQ:(r + 1) * DQ, k, :],
                              kw_sb[r * DQ:(r + 1) * DQ, k, :], start=True, stop=True)
                last.then_inc(S["A_ps"], 1)
            pe.wait_ge(S["consts_ok"], 1)
            for i in range(B // 4):
                pe.wait_ge(S["xn_ok"], 4 * i + 4)
                for j in range(4):
                    last = nc.tensor.transpose(ps[:, PT[i], j * T:(j + 1) * T], xn[:, 4 * i + j, :],
                                               ident[:, :])
                last.then_inc(S["xnT_ps"], 1)
            pe.wait_ge(S["xnT_ok"], B // 4)
            pe.wait_ge(S["A_ok"], NG)

            def t_group(n):
                b, g = divmod(n, NG)
                if n >= 2:
                    pe.wait_ge(S["t_ok"], n - 1)
                if g >= 2:
                    pe.wait_ge(S["v_ok"], 2 * b + g - 1)
                for j in range(GH):
                    last = mm(ps[:, PROJ[n % 2], j * T:(j + 1) * T], A_sb[:, GH * g + j, :], xnT[:, b, :],
                              start=True, stop=True)
                last.then_inc(S["t_ps"], 1)

            def v_proj(b):
                for i in range(2):
                    pe.wait_ge(S["t_ok"], NG * b + i + 1)
                    mm(ps[:, PROJ[i], :], xnT[:, b, :], vw_sb[:, i * 512:(i + 1) * 512],
                       start=True, stop=True).then_inc(S["v_ps"], 1)

            def scores(n):
                b = n // NG
                pe.wait_ge(S["t_ok"], n + 1)
                if n >= 2:
                    pe.wait_ge(S["exp_ok"], n - 1)
                mm(ps[:, SC[n % 2], :], ident_b[:, :], causal[:, :, :].rearrange("p h c -> p (h c)"),
                   start=True, stop=False, skip_group_check=True)
                for j in range(GH):
                    last = mm(ps[:, SC[n % 2], j * T:(j + 1) * T], tT_sb[:, n % 4, j, :], xnT[:, b, :],
                              start=False, stop=True, skip_group_check=True)
                last.then_inc(S["s_ps"], 1)

            def transpose_p(n):
                pe.wait_ge(S["pn_ok"], n + 1)
                if n >= 2:
                    pe.wait_ge(S["pt_ok"], n - 1)
                for j in range(GH):
                    last = nc.tensor.transpose(ps[:, PT[n % 2], j * T:(j + 1) * T], pn_sb[:, n % 3, j, :],
                                               ident[:, :])
                last.then_inc(S["pt_ps"], 1)

            def attend(n):
                b, g = divmod(n, NG)
                pe.wait_ge(S["pt_ok"], n + 1)
                pe.wait_ge(S["v_ok"], 2 * b + 2)
                if n % 2 == 0 and n:
                    pe.wait_ge(S["y_ok"], n // 2)
                for j in range(GH):
                    col = ((n % 2) * 2 + j // 2) * T
                    r = (j % 2) * DV
                    last = mm(ps[r:r + DV, YB, col:col + T], v_sb[:, b % 2, GH * g + j, :],
                              pT_sb[:, n % 3, j, :], start=True, stop=True)
                last.then_inc(S["y_ps"], 1)

            def pre():
                pe.wait_ge(S["ctx_in"], 16)
                pe.wait_ge(S["small_in"], 16 * 7)
                done = 0
                for w, src in ((wkT_sb, ctxT_sb), (wvT_sb, ctxT_sb), (wq_sb, kpT), (bq_bc, kpT)):
                    for h in range(2):
                        pe.wait_ge(S["pre_ok"], done + 1)
                        mm(ps[:, MB, 0:HALF], w[:, :], src[:, h * HALF:(h + 1) * HALF],
                           start=True, stop=True).then_inc(S["pre_ps"], 1)
                        done += 1
                pe.wait_ge(S["pre_ok"], done + 1)
                for i in range(2):
                    if i:
                        pe.wait_ge(S["vo_ok"], i)
                    for j in range(4):
                        b = 4 * i + j
                        last = mm(ps[0:S2, MB, j * D:(j + 1) * D], vpT[:, b * S2:(b + 1) * S2], woT_sb[:, :],
                                  start=True, stop=True)
                    last.then_inc(S["vo_ps"], 1)

            def chain(n, half):
                at = chain_at(n, half)
                if at is None:
                    return
                b, k = at
                if k == "z":
                    pe.wait_ge(S["y_ok"], 2 * b + 2)
                    if b:
                        pe.wait_ge(S["slot_ok"], b)
                    else:
                        pe.wait_ge(S["vo_ok"], 2)
                    for p in range(NP):
                        last = mm(ps[:, MB, 0:D], yT_sb[:, b % 2, p, :], ww_sb[:, p, :],
                                  start=(p == 0), stop=(p == NP - 1))
                    last.then_inc(S["z_ps"], 1)
                elif k == "tr2":
                    pe.wait_ge(S["xn2_ok"], b + 1)
                    nc.tensor.transpose(ps[:, MB, 0:T], xn2[:, :], ident[:, :]).then_inc(S["xn2T_ps"], 1)
                elif k == "sc2":
                    pe.wait_ge(S["xn2T_ok"], b + 1)
                    mm(ps[:, MB, 0:S2], xn2T[:, :], qk2[:, b * S2:(b + 1) * S2],
                       start=True, stop=True).then_inc(S["s2_ps"], 1)
                elif k == "trp2":
                    pe.wait_ge(S["p2_ok"], b + 1)
                    nc.tensor.transpose(ps[0:S2, MB, 0:T], p2[:, :], ident[:, :]).then_inc(S["p2T_ps"], 1)
                elif k == "o2":
                    pe.wait_ge(S["p2T_ok"], b + 1)
                    mm(ps[:, MB, 0:D], p2T[:, :], vo[:, b, :], start=True, stop=True).then_inc(S["o2_ps"], 1)
                elif k == "tr3":
                    pe.wait_ge(S["xn3_ok"], b + 1)
                    nc.tensor.transpose(ps[:, MB, 0:T], rows[:, b, 0, 0:D], ident[:, :]) \
                        .then_inc(S["xn3T_ps"], 1)
                elif k == "lg":
                    pe.wait_ge(S["xn3T_ok"], b + 1)
                    mm(ps[:, MB, 0:E], xn3T[:, :], gw_sb[:, :], start=True, stop=True).then_inc(S["lg_ps"], 1)
                elif k == "pf":
                    pe.wait_ge(S["oh_ok"], b + 1)
                    if b:
                        pe.wait_ge(S["taken_ok"], b)
                    mm(ps[:, MB, 0:2 * E], before[:, :], oh[:, :, :].rearrange("p k e -> p (k e)"),
                       start=True, stop=False)
                    mm(ps[:, MB, 0:2 * E], ones_b[:, :], taken[:, :, :].rearrange("p k e -> p (k e)"),
                       start=False, stop=True).then_inc(S["pf_ps"], 1)

            pe.wait_ge(S["vw_in"], 32)
            pe.wait_ge(S["gate_in"], 16)
            for n in STEPS:
                if n + 2 < G:
                    t_group(n + 2)
                    if (n + 2) % NG == 1:
                        v_proj((n + 2) // NG)
                if 0 <= n + 1 < G:
                    scores(n + 1)
                chain(n, 0)
                if 0 <= n < G:
                    transpose_p(n)
                chain(n, 1)
                if 0 <= n - 1 < G:
                    attend(n - 1)
                if n == 1:
                    pre()

            def dispatch(e):
                pe.wait_ge(rows_in[e], 16 * NT)
                if e >= 2:
                    pe.wait_ge(S["dT_ok"], e - 1)
                for i, (t, m) in enumerate(TILES):
                    last = nc.tensor.transpose(ps[:, DT[e % 2], t:t + m], dsp[0:m, e, i, 0:D],
                                               ident[0:m, 0:m])
                last.then_inc(S["dT_ps"], 1)

            def down(e):
                pe.wait_ge(S["h_ok"], FC * (e + 1))
                if e >= 2:
                    pe.wait_ge(S["eo_ok"], NT * (e - 1))
                for i, (t, m) in enumerate(TILES):
                    for f in range(FC):
                        last = mm(ps[0:m, OUT_B[e % 2], i * D:(i + 1) * D], hT[:, e % 2, f, t:t + m],
                                  wd_sb[:, e, f, :], start=(f == 0), stop=(f == FC - 1))
                last.then_inc(S["o_ps"], 1)

            dispatch(0)
            for e in range(E):
                pe.wait_ge(S["dT_ok"], e + 1)
                pe.wait_ge(ffn_in[e], 48)
                for f in range(FC):
                    i = e * FC + f
                    if i >= 2:
                        pe.wait_ge(S["h_ok"], i - 1)
                    mm(ps[:, GATE[i % 2], 0:SLOTS], wg_sb[:, e, f * P:(f + 1) * P], dT[:, e % 2, :],
                       start=True, stop=True).then_inc(S["g_ps"], 1)
                    mm(ps[:, UP[i % 2], 0:SLOTS], wu_sb[:, e, f * P:(f + 1) * P], dT[:, e % 2, :],
                       start=True, stop=True).then_inc(S["u_ps"], 1)
                    if f == 0 and e + 1 < E:
                        dispatch(e + 1)
                    if f == 1 and e:
                        down(e - 1)
            down(E - 1)


def kernel(**inputs):
    import numpy as _np
    import concourse.bacc as _bacc
    from concourse import mybir as _mybir
    from concourse.bass_utils import run_bass_kernel_spmd as _run

    i = {k: _np.asarray(v) for k, v in inputs.items()}
    B, T, D = i["x"].shape
    DQ, _, H = i["L0_attn_Q"].shape
    DV = i["L0_attn_V"].shape[0]
    E, F, _ = i["L0_ffn_wi_gate"].shape

    def halves(w):
        return w.reshape(DQ, D, 2, H // 2).transpose(2, 0, 3, 1).reshape(2 * DQ, H // 2, D)

    arrays = {
        "x": i["x"],
        "ctxT": i["ctx_1024"].reshape(-1, D).T,
        "q_w": halves(i["L0_attn_Q"]),
        "k_w": halves(i["L0_attn_K"]),
        "v_w": i["L0_attn_V"].transpose(1, 2, 0).reshape(D, H * DV),
        "w_w": i["L0_attn_W"].reshape(D, DV, H // 2, 2).transpose(3, 1, 2, 0).reshape(2 * DV, H // 2, D),
        "wkT": i["L0_xattn_Wk"].T,
        "wvT": i["L0_xattn_Wv"].T,
        "bv": i["L0_xattn_bv"],
        "wq": i["L0_xattn_Wq"],
        "bq": i["L0_xattn_bq"],
        "woT": i["L0_xattn_Wo"].T,
        "bo": i["L0_xattn_bo"],
        "gate_wT": i["L0_ffn_gate_w"].T,
        "wgT": i["L0_ffn_wi_gate"].transpose(2, 0, 1),
        "wuT": i["L0_ffn_wi_up"].transpose(2, 0, 1),
        "wdT": i["L0_ffn_wo"].reshape(E, D, F // 128, 128).transpose(3, 0, 2, 1),
    }
    arrays = {k: _np.ascontiguousarray(v) for k, v in arrays.items()}
    nc = _bacc.Bacc("TRN2", target_bir_lowering=False, num_devices=1)
    args = [nc.dram_tensor(k, v.shape, _mybir.dt.from_np(v.dtype), kind="ExternalInput").ap()
            for k, v in arrays.items()]
    out = nc.dram_tensor("out", (B, T, D), _mybir.dt.float32, kind="ExternalOutput").ap()
    decoder_layer(nc, *args, out)
    r = _run(nc, [arrays], core_ids=[0])
    return r.results[0]["out"]
```

```python
from contextlib import ExitStack

import concourse.bass as bass
from concourse import mybir

F32 = mybir.dt.float32
F32R = mybir.dt.float32r
BF16 = mybir.dt.bfloat16
I32 = mybir.dt.int32
U32 = mybir.dt.uint32
ALU = mybir.AluOpType
ACT = mybir.ActivationFunctionType
AX_X = mybir.AxisListType.X


SCRATCH_ROWS = 3 * 128


def decoder_layer(nc, x, ctxT, q_w, k_w, v_w, w_w, wkT, wvT, bv, wq, bq, woT, bo, gate_wT,
                  wgT, wuT, wdT, out):
    B, T, D = x.shape
    H = 2 * q_w.shape[1]
    DQ = q_w.shape[0] // 2
    DV = v_w.shape[1] // H
    S2 = ctxT.shape[1] // B
    E, F = wgT.shape[1:]
    N = B * T
    CAP = max(int(N / E * 1.25), 1)
    NT = 3
    TILE = 2 * -(-CAP // NT)
    SLOTS = NT * TILE
    P = 128
    assert T == P and D == P and 2 * DV == P and 2 * DQ == P
    GH = 4
    NG = H // GH
    G = B * NG
    NP = H // 2
    FC = F // P
    assert TILE <= P and NT * P == SCRATCH_ROWS
    ROW = D + 2
    EPS = 1e-5
    BIG = 1e30
    A_SCALE = -(DQ / D) / DQ
    Z_SCALE = (DV / D) ** 0.5 * (D / DV) ** 0.5 / H
    X_SCALE = -float(D) ** -0.5
    HALF = B * S2 // 2
    NV = 2
    VC = H * DV // NV
    TH = 2
    NJ = H // TH
    NTP = B // 2 * NJ
    TR = NJ + 2
    WR = 4
    LEAD = NG + 2

    disp = nc.dram_tensor("dispatched_rows", [E * SLOTS + 2 * B * P, ROW], F32).ap()

    with ExitStack() as ctx:
        def sb(name, shape, dt=F32):
            return ctx.enter_context(nc.sbuf_tensor(name, shape, dt))

        def sem(name):
            return ctx.enter_context(nc.semaphore(name))

        x2 = sb("x2", [P, B, D])
        bv_sb = sb("bv_sb", [P, 1])
        bq_sb = sb("bq_sb", [P, 1])
        gw_sb = sb("gw_sb", [P, E])
        gw_centred = sb("gw_centred", [P, E])
        w_raw = sb("w_raw", [P, 2, 3, F])
        w_hi = sb("w_hi", [P, WR, 3, F], F32R)
        w_lo = sb("w_lo", [P, WR, 3, F], F32R)

        ident = sb("ident", [P, P])
        before = sb("before", [P, P], BF16)
        ones_b = sb("ones_b", [P, P], BF16)
        iota_e = sb("iota_e", [P, 2, E])
        dump_row = sb("dump_row", [P, B, 2])
        base_row = sb("base_row", [P, B, 2])
        minus_half = sb("minus_half", [P, B])
        blank = sb("blank", [P, NT, ROW])

        stat1 = sb("stat1", [P, B, 6])
        mv1 = sb("mv1", [P, B, 2])
        rstd1 = sb("rstd1", [P, B])
        smin = sb("smin", [P, 4, GH])
        ssum = sb("ssum", [P, 4, GH])
        sinv = sb("sinv", [P, 4, GH])

        stat = sb("stat", [P, 2, 6])
        mv = sb("mv", [P, 2, 2])
        rstd = sb("rstd", [P, 2])
        s2min = sb("s2min", [P, 1])
        s2sum = sb("s2sum", [P, 1])
        s2inv = sb("s2inv", [P, 1])
        rows = sb("rows", [P, B, 2, ROW])
        x2T = sb("x2T", [P, T])
        diff = sb("diff", [P, 1])
        top8 = sb("top8", [P, 8])
        idx8 = sb("idx8", [P, 8], U32)
        idxf = sb("idxf", [P, 2])
        ratio = sb("ratio", [P, 1])
        denom = sb("denom", [P, 1])
        oh = sb("oh", [P, 2, E], BF16)
        taken = sb("taken", [P, 2, E], BF16)
        sbase = sb("sbase", [P, 2])
        prod = sb("prod", [P, 2, E])
        pos = sb("pos", [P, 2])
        rel = sb("rel", [P, 2])
        relok = sb("relok", [P, 2])
        slot = sb("slot", [P, B, 2], I32)


        with ExitStack() as attention_phase:
            def sb1(name, shape, dt=F32):
                return attention_phase.enter_context(nc.sbuf_tensor(name, shape, dt))

            with ExitStack() as weight_phase:
                def sb0(name, shape, dt=F32):
                    return weight_phase.enter_context(nc.sbuf_tensor(name, shape, dt))

                qw_sb = sb0("qw_sb", [P, H // 2, D])
                kw_sb = sb0("kw_sb", [P, H // 2, D])
            yT_sb = sb1("yT_sb", [P, 2, NP, T])
            x_sb = sb1("x_sb", [P, B, D])
            x1 = sb1("x1", [P, 2, D])
            ctxT_sb = sb1("ctxT_sb", [P, B * S2])
            vw_sb = sb1("vw_sb", [P, H * DV])
            ww_sb = sb1("ww_sb", [P, NP, D])
            wkT_sb = sb1("wkT_sb", [P, D])
            wvT_sb = sb1("wvT_sb", [P, D])
            wq_sb = sb1("wq_sb", [P, D])
            woT_sb = sb1("woT_sb", [P, D])
            bo_bc = sb1("bo_bc", [S2, D])
            vw_hi = sb1("vw_hi", [P, H * DV], F32R)
            vw_lo = sb1("vw_lo", [P, H * DV], F32R)
            xn = sb1("xn", [P, B, D])
            xnT_hi = sb1("xnT_hi", [P, B, T], F32R)
            xnT_lo = sb1("xnT_lo", [P, B, T], F32R)
            kpT = sb1("kpT", [P, B * S2])
            vpT = sb1("vpT", [P, B * S2])
            qk2 = sb1("qk2", [P, B * S2])
            qbias = sb1("qbias", [P, B * S2])
            bq_bc = sb1("bq_bc", [P, P])
            vo = sb1("vo", [S2, B, D])
            causal = sb1("causal", [P, P])
            x1T = sb1("x1T", [P, T])
            centre = sb1("centre", [P, D])
            wq_mean = sb1("wq_mean", [P, 1])
            s2_sb = sb1("s2_sb", [P, S2])
            p2 = sb1("p2", [P, S2])
            p2T = sb1("p2T", [S2, T])
            A_hi = sb1("A_hi", [P, H, D], F32R)
            A_lo = sb1("A_lo", [P, H, D], F32R)
            tT_sb = sb1("tT_sb", [P, TR, TH, 2, T])
            s_sb = sb1("s_sb", [P, 2, GH, T])
            xnT = sb1("xnT", [P, B, T])
            v_sb = sb1("v_sb", [P, 2, H, DV])
            p_sb = sb1("p_sb", [P, 3, GH, T])
            pn_sb = sb1("pn_sb", [P, 2, GH, T])
            pT_sb = sb1("pT_sb", [P, 2, GH, T])

        dsp = sb("dsp", [P, E, NT, ROW])
        dT_hi = sb("dT_hi", [P, 2, SLOTS], F32R)
        dT_lo = sb("dT_lo", [P, 2, SLOTS], F32R)
        sg = sb("sg", [P, 2, SLOTS])
        hT = sb("hT", [P, 2, SLOTS])
        hT_hi = sb("hT_hi", [P, 2, FC, SLOTS], F32R)
        hT_lo = sb("hT_lo", [P, 2, FC, SLOTS], F32R)
        oT = sb("oT", [P, SLOTS])
        eo = sb("eo", [P, 2, NT, D])

        ps = ctx.enter_context(nc.psum_tensor("ps", [P, 8, 512], F32))
        PROJ, SC, PT, YB, MB = [0, 1], [2, 3], 4, 5, [6, 7]
        A_BANK = [PT, YB] + MB
        GATE, UP, DT, OT, OUT_B = [0, 1], [2, 3], 4, [5, 7], 6

        names = """vw_in ctx_in small_in gate_in consts_ok blank_ok blank_out
        mv1_ok rstd1_ok xn_ok xnT_ok xnT_lo_ok A_ps A_hi_ok A_ok vw_hi_ok vw_lo_ok
        proj_ps proj_ok s_ps min_ok exp_ok sinv_ok pn_ok pt_ps pt_ok y_ps y_ok
        bq_ok wq_ok gw_ps gw_ok diff_ok pre_ps pre_ok vo_ps vo_ok za_ps z_ps x1_ok mv2_ok mv3_ok rstd2_ok rstd3_ok s2_ok x1T_ps
        x1T_ok s2_ps s2min_ok s2inv_ok p2_ok p2T_ps p2T_ok o2_ps x2_ok xn3_ok x2T_ps x2T_ok lg_ps
        top_ok ratio_ok wts_ok oh_ok pf_ps taken_ok slot_ok acc_out dve_step pool_step scattered
        w_hi_ok w_lo_ok dT_ps dT_hi_ok dT_ok g_ps u_ps sg_ok h_ok h_hi_ok h_lo_ok oT_ps oT_ok o_ps eo_ok
        added""".split()
        S = {n: sem(n) for n in names}
        qk_in = [sem(f"qk_in{i}") for i in range(2)]
        x_in = [sem(f"x_in{i}") for i in range(B // 2)]
        w_in = [sem(f"w_in{i}") for i in range(2)]
        rows_in = [sem(f"rows_in{e}") for e in range(E)]

        PLACE = dict(za=0, z=2, stat2=3, rstd2=4, tr2=4, x1T=5, sc2=6, min2=7, p2=8, trp2=9,
                     p2T=10, o2=12, stat3=12, rstd3=13, tr3=13, x2T=14, lg=16, choice=16, xn3=17,
                     ratio=18, pf=18, weights=19, slots=20, scatter=21)
        ORDER = dict(pe=["proj", "c0", "scores", "c1", "trp", "c2", "att", "c3"],
                     act=["proj", "c0", "c1", "exps", "c2", "y", "c3"],
                     dve=["c0", "c1", "min", "inv", "pt", "c2", "c3", "hi"],
                     pool=["c0", "norm", "c1", "lo", "c2", "c3"])
        V_LEAD = 1
        PRE_FIRST = 4
        PREP = dict(stats=-8, rstd=-7, norm=-5, low=-1)
        WARM = (8, 20)
        DOWN_LAG = 3
        FC_AFTER = 2 * FC
        AT = dict(rows=-8, hi=-6, lo=-6, out=14, by_row=16, weigh=16)
        PLACE = {'za': 0, 'z': 2, 'stat2': 2, 'rstd2': 4, 'tr2': 3, 'x1T': 4, 'sc2': 6, 'min2': 7, 'p2': 7, 'trp2': 10, 'p2T': 9, 'o2': 13, 'stat3': 13, 'rstd3': 16, 'tr3': 17, 'x2T': 16, 'lg': 19, 'choice': 19, 'xn3': 24, 'ratio': 21, 'pf': 23, 'weights': 24, 'slots': 26, 'scatter': 30}
        ORDER = {'pe': ['proj', 'c0', 'scores', 'c1', 'trp', 'c2', 'att', 'c3'], 'act': ['proj', 'c0', 'c1', 'exps', 'c2', 'y', 'c3'], 'dve': ['c0', 'inv', 'min', 'c1', 'pt', 'c2', 'c3', 'hi'], 'pool': ['c0', 'norm', 'c1', 'c2', 'c3', 'lo']}
        FIRST_CHUNK = 3
        PREP = {'stats': -8, 'rstd': -7, 'norm': -5, 'low': -1}
        PRE_FIRST = 8
        AT = {'rows': -8, 'hi': -6, 'lo': -5, 'out': 14, 'by_row': 16, 'weigh': 16}
        DOWN_LAG = 3
        WARM = [8, 20]

        STEPS = range(-1, G + 3 + max(PLACE.values()) // 4)

        def chain_at(n, place, steps):
            at = 4 * n + place
            found = []
            for b in range(B):
                for k in steps:
                    if 4 * (NG * b + NG + 2) + PLACE[k] == at:
                        found.append((b, k))
            return found

        def projections(n):
            uses = []
            if n < NJ - LEAD:
                uses += [("t", t) for t in (2 * n + 4, 2 * n + 5)]
            elif n + LEAD < NTP:
                uses.append(("t", n + LEAD))
            b, k = divmod(n + V_LEAD, NG)
            if 0 <= b < B and k < NV:
                uses.append(("v", b, k))
            i, k = divmod(n + LEAD + 2, 2 * NG)
            if 1 <= i < B // 2 and k == 0:
                uses.append(("x", i))
            return uses

        def prepared(n, place, step):
            i, at = divmod(4 * (n + LEAD + 1) + place, 8 * NG)
            at -= 8 * NG if at > 4 * NG else 0
            i += 1 if at < 0 else 0
            return i if 1 <= i < B // 2 and at == PREP[step] else None

        USES = [("x", 0), ("t", 0), ("t", 1)] + [u for n in STEPS for u in projections(n)]
        TURN = {u: i for i, u in enumerate(USES)}

        PRE = {PRE_FIRST + i: i for i in range(11)}
        CHUNKS = 3 * WR
        FIRST_CHUNK = 3

        def expert_steps(at, steps):
            for name, step in steps:
                e, rest = divmod(at - AT[name], 2 * FC)
                if rest == 0 and 0 <= e < E and (e or AT[name] >= 0):
                    step(e)

        block = ctx.enter_context(nc.Block())

        @block.sync
        def _(sp):
            def load_x(i):
                sp.dma_start(x_sb[:, 2 * i:2 * i + 2, :], x[2 * i:2 * i + 2].rearrange("b t d -> t b d")) \
                    .then_inc(x_in[i], 16)

            load_x(0)
            for i in range(2):
                half = slice(i * NP // 2, (i + 1) * NP // 2)
                sp.dma_start(kw_sb[:, half, :], k_w[:, half, :]).then_inc(qk_in[i], 16)
            sp.dma_start(vw_sb[:, :], v_w).then_inc(S["vw_in"], 16)
            load_x(1)
            sp.dma_start(ctxT_sb[:, :], ctxT).then_inc(S["ctx_in"], 16)
            for dst, src in ((wkT_sb, wkT), (wvT_sb, wvT), (wq_sb, wq), (woT_sb, woT),
                             (bv_sb, bv.rearrange("(p a) -> p a", a=1)),
                             (bq_sb, bq.rearrange("(p a) -> p a", a=1)),
                             (bo_bc, bo.rearrange("(a d) -> a d", a=1).to_broadcast([S2, D]))):
                sp.dma_start(dst[:, :], src).then_inc(S["small_in"], 16)
            sp.dma_start(ww_sb[:, :, :], w_w).then_inc(S["gate_in"], 16)
            sp.dma_start(gw_sb[:, :], gate_wT).then_inc(S["gate_in"], 16)
            load_x(2)
            load_x(3)

            def load_expert(e):
                if e >= 2:
                    sp.wait_ge(S["w_hi_ok"], 3 * (e - 1))
                    sp.wait_ge(S["w_lo_ok"], 3 * (e - 1))
                sp.dma_start(w_raw[:, e % 2, 0, :], wgT[:, e, :]).then_inc(w_in[e % 2], 16)
                sp.dma_start(w_raw[:, e % 2, 1, :], wuT[:, e, :]).then_inc(w_in[e % 2], 16)
                sp.dma_start(w_raw[:, e % 2, 2, :], wdT[:, e, :, :].rearrange("p f d -> p (f d)")) \
                    .then_inc(w_in[e % 2], 16)

            load_expert(0)
            load_expert(1)
            sp.wait_ge(S["blank_ok"], 2)
            rows_of = disp[0:E * SLOTS, :].rearrange("(e s) r -> s e r", e=E)
            for i in range(NT):
                sp.dma_start(rows_of[i * TILE:(i + 1) * TILE],
                             blank[0:TILE, i, :].unsqueeze(1).to_broadcast([TILE, E, ROW])) \
                    .then_inc(S["blank_out"], 16)
            sp.dma_start(out[N:N + NT * P, :].rearrange("(t p) d -> p t d", p=P), blank[:, :, 0:D]) \
                .then_inc(S["blank_out"], 16)
            for b in range(B):
                if b + 2 < WR + 2:
                    load_expert(b + 2)
                sp.wait_ge(S["x2_ok"], b + 1)
                sp.dma_start(out[b * T:(b + 1) * T, :], x2[:, b, :]).then_inc(S["acc_out"], 16)
            sp.wait_ge(S["scattered"], 2 * B * 16)
            for e in range(E):
                sp.dma_start(dsp[0:TILE, e, :, :],
                             disp[e * SLOTS:(e + 1) * SLOTS, :].rearrange("(p t) r -> p t r", t=NT)) \
                    .then_inc(rows_in[e], 16)
            for e in range(WR + 2, E):
                load_expert(e)
            sp.wait_ge(S["added"], 16 * NT * E)

        @block.gpsimd
        def _(pool):
            g = nc.gpsimd
            n_link = [0]

            def link(ins):
                n_link[0] += 1
                ins.then_inc(S["pool_step"], 1)
                pool.wait_ge(S["pool_step"], n_link[0])

            g.memset(minus_half[:, :], -0.5)
            link(g.memset(ident[:, :], 0.0))
            g.affine_select(out=ident[:, :], in_=ident[:, :], compare_op=ALU.not_equal, fill=1.0,
                            base=0, pattern=[[-1, P]], channel_multiplier=1)
            link(g.memset(causal[:, :], 0.0))
            g.affine_select(out=causal[:, :], in_=causal[:, :], compare_op=ALU.is_ge, fill=BIG,
                            base=0, pattern=[[-1, P]], channel_multiplier=1).then_inc(S["consts_ok"], 1)

            def rstd_1(i):
                pool.wait_ge(S["mv1_ok"], i + 1)
                two = rstd1[:, 2 * i:2 * i + 2]
                link(g.tensor_scalar(two, mv1[:, 2 * i:2 * i + 2, 1], EPS, None, ALU.add))
                g.tensor_tensor(two, two, minus_half[:, 0:2], ALU.pow).then_inc(S["rstd1_ok"], 1)

            rstd_1(0)
            g.tensor_scalar(centre[:, :], ident[:, :], -1.0 / D, None, ALU.add).then_inc(S["consts_ok"], 1)
            for i in range(NV):
                pool.wait_ge(S["vw_hi_ok"], i + 1)
                cols = slice(i * VC, (i + 1) * VC)
                g.tensor_tensor(vw_lo[:, cols], vw_sb[:, cols], vw_hi[:, cols].bitcast(F32), ALU.subtract) \
                    .then_inc(S["vw_lo_ok"], 1)
            link(g.memset(before[:, :], 1.0))
            g.affine_select(out=before[:, :], in_=before[:, :], compare_op=ALU.is_ge, fill=0.0,
                            base=-1, pattern=[[1, P]], channel_multiplier=-1)
            g.memset(ones_b[:, :], 1.0)
            g.iota(iota_e[:, :, :], pattern=[[0, 2], [1, E]], base=0, channel_multiplier=0,
                   allow_small_or_imprecise_dtypes=True)
            g.iota(dump_row[:, :, :], pattern=[[2 * P, B], [P, 2]], base=E * SLOTS, channel_multiplier=1,
                   allow_small_or_imprecise_dtypes=True)
            g.iota(base_row[:, :, :], pattern=[[-2 * P, B], [CAP - P, 2]], base=-E * SLOTS,
                   channel_multiplier=-1, allow_small_or_imprecise_dtypes=True)
            g.memset(taken[:, :, :], 0.0)
            g.iota(rows[:, :, :, D + 1].bitcast(I32), pattern=[[T, B], [0, 2]], base=0,
                   channel_multiplier=1)
            g.memset(blank[:, :, 0:D + 1], 0.0).then_inc(S["blank_ok"], 1)
            g.iota(blank[:, :, D + 1].bitcast(I32), pattern=[[P, NT]], base=N,
                   channel_multiplier=1).then_inc(S["blank_ok"], 1)
            def split_lo(i):
                e, k = divmod(i, 3)
                pool.wait_ge(S["w_hi_ok"], i + 1)
                g.tensor_tensor(w_lo[:, e % WR, k, :], w_raw[:, e % 2, k, :], w_hi[:, e % WR, k, :].bitcast(F32),
                                ALU.subtract).then_inc(S["w_lo_ok"], 1)

            def rstd_of(k, b):
                pool.wait_ge(S[f"mv{2 + k}_ok"], b + 1)
                if k and b:
                    pool.wait_ge(S["ratio_ok"], b)
                one = rstd[:, k:k + 1]
                link(g.tensor_scalar(one, mv[:, k, 1:2], EPS, None, ALU.add))
                g.tensor_tensor(one, one, minus_half[:, 0:1], ALU.pow).then_inc(S[f"rstd{2 + k}_ok"], 1)

            def chain(n, place):
                i = prepared(n, place, "rstd")
                if i is not None:
                    rstd_1(i)
                for b, k in chain_at(n, place, ("rstd2", "rstd3", "scatter")):
                    if k == "rstd2":
                        rstd_of(0, b)
                    elif k == "rstd3":
                        rstd_of(1, b)
                    else:
                        if b == 0:
                            pool.wait_ge(S["blank_out"], 16 * 4)
                        pool.wait_ge(S["slot_ok"], b + 1)
                        for c in range(2):
                            pool.indirect_dma_start(
                                out=disp, out_offset=bass.IndirectOffsetOnAxis(ap=slot[:, b, c:c + 1], axis=0),
                                in_=rows[:, b, c, :], in_offset=None).then_inc(S["scattered"], 16)

            for n in STEPS:
                for it in ORDER["pool"]:
                    if it == "norm" and 0 <= n < G:
                        pool.wait_ge(S["sinv_ok"], n + 1)
                        if n >= 2:
                            pool.wait_ge(S["pt_ps"], n - 1)
                        g.tensor_tensor(pn_sb[:, n % 2, :, :], p_sb[:, n % 3, :, :],
                                        sinv[:, n % 4, :].unsqueeze(2).to_broadcast([P, GH, T]), ALU.mult) \
                            .then_inc(S["pn_ok"], 1)
                    elif it == "lo" and 0 <= n - FIRST_CHUNK < CHUNKS:
                        split_lo(n - FIRST_CHUNK)
                    elif it[0] == "c":
                        chain(n, int(it[1]))

            pool.wait_ge(S["acc_out"], 16 * B)
            for e in range(E):
                if 1 <= e <= E - WR:
                    for k in range(3):
                        split_lo(3 * (e - 1 + WR) + k)
                pool.wait_ge(S["eo_ok"], NT * (e + 1))
                if e:
                    pool.wait_ge(S["added"], 16 * NT * e)
                for i in range(NT):
                    pool.indirect_dma_start(
                        out=out, out_offset=bass.IndirectOffsetOnAxis(
                            ap=dsp[0:TILE, e, i, D + 1:D + 2].bitcast(I32), axis=0),
                        in_=eo[0:TILE, e % 2, i, :], in_offset=None, compute_op=ALU.add) \
                        .then_inc(S["added"], 16)

        @block.scalar
        def _(act):
            a = nc.scalar
            for i in range(2):
                half = slice(i * NP // 2, (i + 1) * NP // 2)
                act.dma_start(qw_sb[:, half, :], q_w[:, half, :]).then_inc(qk_in[i], 16)

            def high_A(i):
                act.wait_ge(S["A_ps"], 2 * (i // 2 + 1))
                a.activation(A_hi[:, GH * i:GH * i + GH, :], ps[:, A_BANK[i], :], ACT.Copy,
                             scale=A_SCALE).then_inc(S["A_hi_ok"], 1)

            def copy_projection(u):
                act.wait_ge(S["proj_ps"], TURN[u] + 1)
                src = ps[:, PROJ[TURN[u] % 2], :]
                if u[0] == "x":
                    a.copy(xnT_hi[:, 2 * u[1]:2 * u[1] + 2, :], src[:, 0:2 * T]).then_inc(S["proj_ok"], 1)
                    return
                if u[0] == "t":
                    if u[1] >= TR:
                        p, j = divmod(u[1] - TR, NJ)
                        act.wait_ge(S["s_ps"], NG * (2 * p + 1) + TH * j // GH + 1)
                    dst = tT_sb[:, u[1] % TR, :, :, :]
                else:
                    _, b, i = u
                    if b >= 2:
                        act.wait_ge(S["y_ps"], NG * (b - 1))
                    dst = v_sb[:, b % 2, i * (H // NV):(i + 1) * (H // NV), :]
                a.copy(dst, src).then_inc(S["proj_ok"], 1)

            def copy_y(i):
                b, k = divmod(i, 2)
                act.wait_ge(S["y_ps"], 2 * i + 2)
                if b >= 2:
                    act.wait_ge(S["z_ps"], b - 1)
                a.copy(yT_sb[:, b % 2, 4 * k:4 * k + 4, :], ps[:, YB, :]).then_inc(S["y_ok"], 1)

            def exps(n):
                act.wait_ge(S["min_ok"], n + 1)
                if n >= 3:
                    act.wait_ge(S["pn_ok"], n - 2)
                if n >= 4:
                    act.wait_ge(S["sinv_ok"], n - 3)
                for h in range(GH):
                    last = a.activation(p_sb[:, n % 3, h, :], s_sb[:, n % 2, h, :], ACT.Exp,
                                        bias=smin[:, n % 4, h:h + 1], scale=-1.0,
                                        accum_out=ssum[:, n % 4, h:h + 1])
                last.then_inc(S["exp_ok"], 1)

            def chain(n, place):
                for b, k in chain_at(n, place, ("x1T", "p2", "p2T", "x2T", "ratio")):
                    m = MB[b % 2]
                    if k == "x1T":
                        act.wait_ge(S["x1T_ps"], b + 1)
                        a.copy(x1T[:, :], ps[:, m, 0:T]).then_inc(S["x1T_ok"], 1)
                    elif k == "p2":
                        act.wait_ge(S["s2min_ok"], b + 1)
                        a.activation(p2[:, :], s2_sb[:, :], ACT.Exp, bias=s2min[:, :], scale=-1.0,
                                     accum_out=s2sum[:, :]).then_inc(S["p2_ok"], 1)
                    elif k == "p2T":
                        act.wait_ge(S["p2T_ps"], b + 1)
                        a.copy(p2T[:, :], ps[0:S2, m, 0:T]).then_inc(S["p2T_ok"], 1)
                    elif k == "x2T":
                        act.wait_ge(S["x2T_ps"], b + 1)
                        a.copy(x2T[:, :], ps[:, m, 0:T]).then_inc(S["x2T_ok"], 1)
                    else:
                        act.wait_ge(S["diff_ok"], b + 1)
                        act.wait_ge(S["rstd3_ok"], b + 1)
                        a.activation(ratio[:, :], diff[:, :], ACT.Exp, scale=rstd[:, 1:2]) \
                            .then_inc(S["ratio_ok"], 1)

            copy_projection(("x", 0))
            act.wait_ge(S["vw_in"], 16)
            for i in range(NV):
                a.copy(vw_hi[:, i * VC:(i + 1) * VC], vw_sb[:, i * VC:(i + 1) * VC]).then_inc(S["vw_hi_ok"], 1)
            high_A(0)
            high_A(1)
            copy_projection(("t", 0))
            copy_projection(("t", 1))
            high_A(2)
            high_A(3)
            for n in STEPS:
                for it in ORDER["act"]:
                    if it == "proj":
                        for u in projections(n):
                            copy_projection(u)
                    elif it == "exps" and 0 <= n + 1 < G:
                        exps(n + 1)
                    elif it == "y" and 0 <= n - 2 < G and n % 2:
                        copy_y((n - 2) // 2)
                    elif it[0] == "c":
                        chain(n, int(it[1]))

            def dispatch_hi(e):
                act.wait_ge(S["dT_ps"], e + 1)
                if e >= 2:
                    act.wait_ge(S["u_ps"], FC * (e - 1))
                a.copy(dT_hi[:, e % 2, :], ps[:, DT, 0:SLOTS]).then_inc(S["dT_hi_ok"], 1)

            def out_of(e):
                act.wait_ge(S["oT_ps"], e + 1)
                if e:
                    act.wait_ge(S["o_ps"], e)
                a.copy(oT[:, :], ps[:, OT[e % 2], 0:SLOTS]).then_inc(S["oT_ok"], 1)

            def weigh(e):
                act.wait_ge(S["o_ps"], e + 1)
                if e >= 2:
                    act.wait_ge(S["added"], 16 * NT * (e - 1))
                for i in range(NT):
                    a.activation(eo[0:TILE, e % 2, i, :], ps[0:TILE, OUT_B, i * D:(i + 1) * D],
                                 ACT.Copy, scale=dsp[0:TILE, e, i, D:D + 1]).then_inc(S["eo_ok"], 1)

            dispatch_hi(0)
            for i in range(E * FC + FC_AFTER):
                e, f = divmod(i, FC)
                if e < E:
                    act.wait_ge(S["g_ps"], i + 1)
                    if i >= 2:
                        act.wait_ge(S["h_ok"], i - 1)
                    a.activation(sg[:, i % 2, :], ps[:, GATE[i % 2], 0:SLOTS], ACT.Silu) \
                        .then_inc(S["sg_ok"], 1)
                expert_steps(2 * i, (("hi", dispatch_hi), ("out", out_of), ("weigh", weigh)))
                if e < E:
                    act.wait_ge(S["h_ok"], i + 1)
                    if e >= 2:
                        act.wait_ge(S["oT_ps"], e - 1)
                    a.copy(hT_hi[:, e % 2, f, :], hT[:, i % 2, :]).then_inc(S["h_hi_ok"], 1)
                expert_steps(2 * i + 1, (("hi", dispatch_hi), ("out", out_of), ("weigh", weigh)))

        @block.vector
        def _(dve):
            v = nc.vector
            n_link = [0]

            def link(ins):
                n_link[0] += 1
                ins.then_inc(S["dve_step"], 1)
                dve.wait_ge(S["dve_step"], n_link[0])

            def layer_norm_1(i):
                dve.wait_ge(x_in[i], 16)
                for b in (2 * i, 2 * i + 1):
                    ins = v.bn_stats(stat1[:, b, :], x_sb[:, b, :])
                link(ins)
                for b in (2 * i, 2 * i + 1):
                    last = v.bn_aggr(mv1[:, b, :], stat1[:, b, :])
                last.then_inc(S["mv1_ok"], 1)

            def normed_1(i):
                dve.wait_ge(S["rstd1_ok"], i + 1)
                dve.wait_ge(S["mv1_ok"], i + 1)
                for b in (2 * i, 2 * i + 1):
                    last = v.tensor_scalar(xn[:, b, :], x_sb[:, b, :], mv1[:, b, 0:1], rstd1[:, b:b + 1],
                                           ALU.subtract, ALU.mult)
                last.then_inc(S["xn_ok"], 1)

            def transposed_1(i):
                dve.wait_ge(S["proj_ok"], TURN["x", i] + 1)
                src = ps[:, PROJ[TURN["x", i] % 2], 0:2 * T]
                two = xnT_hi[:, 2 * i:2 * i + 2, :].bitcast(F32).rearrange("p b t -> p (b t)")
                v.tensor_tensor(xnT_lo[:, 2 * i:2 * i + 2, :].rearrange("p b t -> p (b t)"), src, two,
                                ALU.subtract).then_inc(S["xnT_lo_ok"], 1)
                v.tensor_copy(xnT[:, 2 * i:2 * i + 2, :].rearrange("p b t -> p (b t)"), src) \
                    .then_inc(S["xnT_ok"], 1)

            def low_A(i):
                dve.wait_ge(S["A_hi_ok"], i + 1)
                v.scalar_tensor_tensor(out=A_lo[:, GH * i:GH * i + GH, :].rearrange("p h d -> p (h d)"),
                                       in0=ps[:, A_BANK[i], :], scalar=A_SCALE,
                                       in1=A_hi[:, GH * i:GH * i + GH, :].bitcast(F32)
                                       .rearrange("p h d -> p (h d)"),
                                       op0=ALU.mult, op1=ALU.subtract).then_inc(S["A_ok"], 1)

            layer_norm_1(0)
            normed_1(0)
            transposed_1(0)
            for i in range(NG):
                low_A(i)

            def row_min(n):
                dve.wait_ge(S["s_ps"], n + 1)
                if n >= 2:
                    dve.wait_ge(S["exp_ok"], n - 1)
                for h in range(GH):
                    last = v.tensor_tensor_reduce(out=s_sb[:, n % 2, h, :], in0=ps[:, SC[n % 2], h * T:(h + 1) * T],
                                                  in1=causal[:, :], scale=1.0, scalar=3e38,
                                                  op0=ALU.add, op1=ALU.min, accum_out=smin[:, n % 4, h:h + 1])
                last.then_inc(S["min_ok"], 1)

            def inverse(n):
                dve.wait_ge(S["exp_ok"], n + 1)
                if n >= 4:
                    dve.wait_ge(S["pn_ok"], n - 3)
                v.reciprocal(sinv[:, n % 4, :], ssum[:, n % 4, :]).then_inc(S["sinv_ok"], 1)

            def copy_pt(n):
                dve.wait_ge(S["pt_ps"], n + 1)
                if n >= 2:
                    dve.wait_ge(S["y_ps"], n - 1)
                v.tensor_copy(pT_sb[:, n % 2, :, :], ps[:, PT, :]).then_inc(S["pt_ok"], 1)

            def pre_copy(i):
                dve.wait_ge(S["pre_ps"], i + 1)
                k, h = divmod(i, 2)
                cols = slice(h * HALF, (h + 1) * HALF)
                src = ps[:, MB[i % 2], 0:HALF]
                if k == 0:
                    ins = v.tensor_scalar(kpT[:, cols], src, X_SCALE, None, ALU.mult)
                elif k == 1:
                    ins = v.tensor_scalar(vpT[:, cols], src, bv_sb[:, 0:1], None, ALU.add)
                elif k == 2:
                    ins = v.tensor_copy(qk2[:, cols], src)
                else:
                    ins = v.tensor_copy(qbias[:, cols], src)
                ins.then_inc(S["pre_ok"], 1)

            def pre_vo(i):
                dve.wait_ge(S["vo_ps"], i + 1)
                v.tensor_tensor(vo[:, 4 * i:4 * i + 4, :], ps[0:S2, MB[i], :].rearrange("p (b d) -> p b d", b=4),
                                bo_bc[:, :].unsqueeze(1).to_broadcast([S2, 4, D]), ALU.add) \
                    .then_inc(S["vo_ok"], 1)

            def stats(k, src):
                link(v.bn_stats(stat[:, k, :], src))
                v.bn_aggr(mv[:, k, :], stat[:, k, :]).then_inc(S[f"mv{2 + k}_ok"], 1)

            def chain(n, place):
                for k, step in (("stats", layer_norm_1), ("norm", normed_1), ("low", transposed_1)):
                    i = prepared(n, place, k)
                    if i is not None:
                        step(i)
                for b, k in chain_at(n, place, ("stat2", "min2", "trp2", "stat3", "xn3", "choice",
                                                "weights", "slots")):
                    chain_step(b, k)

            def chain_step(b, k):
                m = MB[b % 2]
                if k == "stat2":
                    dve.wait_ge(S["z_ps"], b + 1)
                    v.scalar_tensor_tensor(out=x1[:, b % 2, :], in0=ps[:, m, 0:D], scalar=Z_SCALE,
                                           in1=x_sb[:, b, :], op0=ALU.mult, op1=ALU.add) \
                        .then_inc(S["x1_ok"], 1)
                    dve.wait_ge(S["x1_ok"], b + 1)
                    stats(0, x1[:, b % 2, :])
                elif k == "min2":
                    dve.wait_ge(S["s2_ps"], b + 1)
                    if b:
                        dve.wait_ge(S["p2_ok"], b)
                    dve.wait_ge(S["rstd2_ok"], b + 1)
                    v.scalar_tensor_tensor(out=s2_sb[:, :], in0=ps[:, m, 0:S2], scalar=rstd[:, 0:1],
                                           in1=qbias[:, b * S2:(b + 1) * S2], op0=ALU.mult, op1=ALU.add) \
                        .then_inc(S["s2_ok"], 1)
                    dve.wait_ge(S["s2_ok"], b + 1)
                    v.tensor_reduce(s2min[:, :], s2_sb[:, :], axis=AX_X, op=ALU.min) \
                        .then_inc(S["s2min_ok"], 1)
                elif k == "trp2":
                    dve.wait_ge(S["p2_ok"], b + 1)
                    v.reciprocal(s2inv[:, :], s2sum[:, :]).then_inc(S["s2inv_ok"], 1)
                elif k == "stat3":
                    dve.wait_ge(S["o2_ps"], b + 1)
                    dve.wait_ge(S["s2inv_ok"], b + 1)
                    v.scalar_tensor_tensor(out=x2[:, b, :], in0=ps[:, m, 0:D], scalar=s2inv[:, 0:1],
                                           in1=x1[:, b % 2, :], op0=ALU.mult, op1=ALU.add) \
                        .then_inc(S["x2_ok"], 1)
                    dve.wait_ge(S["x2_ok"], b + 1)
                    stats(1, x2[:, b, :])
                elif k == "xn3":
                    dve.wait_ge(S["rstd3_ok"], b + 1)
                    v.tensor_scalar(rows[:, b, :, 0:D], x2[:, b, :].unsqueeze(1).to_broadcast([P, 2, D]),
                                    mv[:, 1, 0:1], rstd[:, 1:2], ALU.subtract, ALU.mult) \
                        .then_inc(S["xn3_ok"], 1)
                elif k == "choice":
                    dve.wait_ge(S["lg_ps"], b + 1)
                    if b:
                        dve.wait_ge(S["ratio_ok"], b)
                    v.max(top8[:, :], ps[:, m, 0:E]).then_inc(S["top_ok"], 1)
                    dve.wait_ge(S["top_ok"], b + 1)
                    v.tensor_tensor(diff[:, :], top8[:, 1:2], top8[:, 0:1], ALU.subtract) \
                        .then_inc(S["diff_ok"], 1)
                    link(v.max_index(idx8[:, :], top8[:, :], ps[:, m, 0:E]))
                    link(v.tensor_copy(idxf[:, :], idx8[:, 0:2]))
                    v.tensor_tensor(oh[:, :, :], iota_e[:, :, :], idxf[:, :].unsqueeze(2).to_broadcast([P, 2, E]),
                                    ALU.is_equal).then_inc(S["oh_ok"], 1)
                elif k == "weights":
                    v.scalar_tensor_tensor(out=sbase[:, :], in0=idxf[:, :], scalar=float(SLOTS),
                                           in1=base_row[:, b, :], op0=ALU.mult, op1=ALU.add)
                    dve.wait_ge(S["ratio_ok"], b + 1)
                    link(v.tensor_scalar(denom[:, :], ratio[:, :], 1.0, None, ALU.add))
                    link(v.reciprocal(rows[:, b, 0, D:D + 1], denom[:, :]))
                    v.tensor_tensor(rows[:, b, 1, D:D + 1], ratio[:, :], rows[:, b, 0, D:D + 1], ALU.mult) \
                        .then_inc(S["wts_ok"], 1)
                elif k == "slots":
                    dve.wait_ge(S["pf_ps"], b + 1)
                    dve.wait_ge(S["oh_ok"], b + 1)
                    link(v.tensor_tensor(prod[:, :, :], ps[:, m, 0:2 * E].rearrange("p (k e) -> p k e", k=2),
                                         oh[:, :, :], ALU.mult))
                    v.tensor_tensor(taken[:, :, :], taken[:, :, :], oh[:, :, :], ALU.add) \
                        .then_inc(S["taken_ok"], 1)
                    link(v.tensor_reduce(pos[:, :], prod[:, :, :], axis=AX_X, op=ALU.add))
                    link(v.tensor_tensor(rel[:, :], pos[:, :], sbase[:, :], ALU.add))
                    link(v.scalar_tensor_tensor(out=relok[:, :], in0=pos[:, :], scalar=float(CAP),
                                                in1=rel[:, :], op0=ALU.is_lt, op1=ALU.mult))
                    dve.wait_ge(S["wts_ok"], b + 1)
                    v.tensor_tensor(slot[:, b, :], relok[:, :], dump_row[:, b, :], ALU.add) \
                        .then_inc(S["slot_ok"], 1)

            def split_hi(i):
                e, k = divmod(i, 3)
                dve.wait_ge(w_in[e % 2], 48 * (e // 2 + 1))
                if e >= WR:
                    dve.wait_ge(S["oT_ps"], e - WR + 1)
                v.tensor_copy(w_hi[:, e % WR, k, :], w_raw[:, e % 2, k, :]).then_inc(S["w_hi_ok"], 1)

            def context(n, place):
                i = PRE.get(4 * n + place, -1)
                if i == 0:
                    dve.wait_ge(S["small_in"], 16 * 7)
                    link(v.tensor_reduce(wq_mean[:, :], wq_sb[:, :], axis=AX_X, op=ALU.add))
                    link(v.tensor_scalar(wq_mean[:, :], wq_mean[:, :], 1.0 / D, None, ALU.mult))
                    v.tensor_scalar(wq_sb[:, :], wq_sb[:, :], wq_mean[:, 0:1], None, ALU.subtract) \
                        .then_inc(S["wq_ok"], 1)
                    v.tensor_copy(bq_bc[:, :], bq_sb[:, 0:1].to_broadcast([P, P])).then_inc(S["bq_ok"], 1)
                if 0 <= i < 8:
                    pre_copy(i)
                elif 8 <= i < 10:
                    pre_vo(i - 8)
                elif i == 10:
                    dve.wait_ge(S["gw_ps"], 1)
                    v.tensor_copy(gw_centred[:, :], ps[:, MB[0], 0:E]).then_inc(S["gw_ok"], 1)

            for n in STEPS:
                for it in ORDER["dve"]:
                    if it == "min" and 0 <= n + 1 < G:
                        row_min(n + 1)
                    elif it == "inv" and 0 <= n < G:
                        inverse(n)
                    elif it == "pt" and 0 <= n - 1 < G:
                        copy_pt(n - 1)
                    elif it == "hi" and 0 <= n - FIRST_CHUNK + 1 < CHUNKS:
                        split_hi(n - FIRST_CHUNK + 1)
                    elif it[0] == "c":
                        chain(n, int(it[1]))
                        context(n, int(it[1]))

            def dispatch_lo(e):
                dve.wait_ge(S["dT_hi_ok"], e + 1)
                v.tensor_tensor(dT_lo[:, e % 2, :], ps[:, DT, 0:SLOTS], dT_hi[:, e % 2, :].bitcast(F32),
                                ALU.subtract).then_inc(S["dT_ok"], 1)

            def hidden_lo(i):
                e, f = divmod(i, FC)
                dve.wait_ge(S["h_hi_ok"], i + 1)
                v.tensor_tensor(hT_lo[:, e % 2, f, :], hT[:, i % 2, :], hT_hi[:, e % 2, f, :].bitcast(F32),
                                ALU.subtract).then_inc(S["h_lo_ok"], 1)

            dispatch_lo(0)
            for i in range(E * FC + 1):
                if i < E * FC:
                    dve.wait_ge(S["sg_ok"], i + 1)
                    dve.wait_ge(S["u_ps"], i + 1)
                    if i >= 2:
                        dve.wait_ge(S["h_lo_ok"], i - 1)
                    v.tensor_tensor(hT[:, i % 2, :], ps[:, UP[i % 2], 0:SLOTS], sg[:, i % 2, :], ALU.mult) \
                        .then_inc(S["h_ok"], 1)
                expert_steps(2 * i, (("lo", dispatch_lo),))
                if i:
                    hidden_lo(i - 1)
                expert_steps(2 * i + 1, (("lo", dispatch_lo),))
                e, k = divmod(i - (2 * FC - 1), FC)
                if 0 <= e < E - WR and k < 3:
                    split_hi(3 * (e + WR) + k)

        @block.tensor
        def _(pe):
            mm = nc.tensor.matmul
            def fold(c):
                pe.wait_ge(qk_in[c], 32)
                for j in range(GH):
                    for r in range(2):
                        k = GH * c + j
                        ins = mm(ps[:, A_BANK[2 * c + r], j * D:(j + 1) * D], qw_sb[r * DQ:(r + 1) * DQ, k, :],
                                 kw_sb[r * DQ:(r + 1) * DQ, k, :], start=True, stop=True)
                        if j == GH - 1:
                            ins.then_inc(S["A_ps"], 1)

            def split_mm(out_ap, w_hi_ap, w_lo_ap, m_hi_ap, m_lo_ap, start=True, stop=True):
                mm(out_ap, w_hi_ap, m_lo_ap, start=start, stop=False)
                mm(out_ap, w_hi_ap, m_hi_ap, start=False, stop=False)
                return mm(out_ap, w_lo_ap, m_hi_ap, start=False, stop=stop)

            def project(u):
                turn = TURN[u]
                if turn >= 2:
                    pe.wait_ge(S["proj_ok"], turn - 1)
                    if USES[turn - 2][0] == "x":
                        pe.wait_ge(S["xnT_ok"], USES[turn - 2][1] + 1)
                bank = ps[:, PROJ[turn % 2], :]
                if u[0] == "x":
                    pe.wait_ge(S["consts_ok"], 1)
                    pe.wait_ge(S["xn_ok"], u[1] + 1)
                    for j in range(2):
                        last = nc.tensor.transpose(bank[:, j * T:(j + 1) * T], xn[:, 2 * u[1] + j, :],
                                                   ident[:, :])
                    last.then_inc(S["proj_ps"], 1)
                    return
                if u[0] == "t":
                    p, j = divmod(u[1], NJ)
                    pe.wait_ge(S["xnT_lo_ok"], p + 1)
                    pe.wait_ge(S["A_ok"], TH * j // GH + 1)
                    for h in range(TH):
                        head = TH * j + h
                        last = split_mm(bank[:, h * 2 * T:(h + 1) * 2 * T], A_hi[:, head, :], A_lo[:, head, :],
                                        xnT_hi[:, 2 * p:2 * p + 2, :].rearrange("p b t -> p (b t)"),
                                        xnT_lo[:, 2 * p:2 * p + 2, :].rearrange("p b t -> p (b t)"))
                else:
                    _, b, i = u
                    pe.wait_ge(S["vw_lo_ok"], i + 1)
                    cols = slice(i * VC, (i + 1) * VC)
                    last = split_mm(bank, xnT_hi[:, b, :], xnT_lo[:, b, :], vw_hi[:, cols], vw_lo[:, cols])
                last.then_inc(S["proj_ps"], 1)

            def scores(n):
                b, g = divmod(n, NG)
                pe.wait_ge(S["proj_ok"], TURN["t", NJ * (b // 2) + GH * (g + 1) // TH - 1] + 1)
                pe.wait_ge(S["xnT_ok"], b // 2 + 1)
                if n >= 2:
                    pe.wait_ge(S["min_ok"], n - 1)
                for j in range(GH):
                    t = NJ * (b // 2) + (GH * g + j) // TH
                    last = mm(ps[:, SC[n % 2], j * T:(j + 1) * T], tT_sb[:, t % TR, j % TH, b % 2, :],
                              xnT[:, b, :], start=True, stop=True)
                last.then_inc(S["s_ps"], 1)

            def transpose_p(n):
                pe.wait_ge(S["pn_ok"], n + 1)
                if n:
                    pe.wait_ge(S["pt_ok"], n)
                else:
                    pe.wait_ge(S["A_ok"], A_BANK.index(PT) + 1)
                for j in range(GH):
                    last = nc.tensor.transpose(ps[:, PT, j * T:(j + 1) * T], pn_sb[:, n % 2, j, :],
                                               ident[:, :])
                last.then_inc(S["pt_ps"], 1)

            def attend(n):
                b, g = divmod(n, NG)
                pe.wait_ge(S["pt_ok"], n + 1)
                pe.wait_ge(S["proj_ok"], TURN["v", b, NV - 1] + 1)
                if n == 0:
                    pe.wait_ge(S["A_ok"], A_BANK.index(YB) + 1)
                elif n % 2 == 0:
                    pe.wait_ge(S["y_ok"], n // 2)
                for j in range(GH):
                    col = ((n % 2) * 2 + j // 2) * T
                    r = (j % 2) * DV
                    last = mm(ps[r:r + DV, YB, col:col + T], v_sb[:, b % 2, GH * g + j, :],
                              pT_sb[:, n % 2, j, :], start=True, stop=True)
                last.then_inc(S["y_ps"], 1)

            def context(n, place):
                i = PRE.get(4 * n + place, -1)
                k, h = divmod(i, 2)
                if 0 <= i < 8:
                    if i == 0:
                        pe.wait_ge(S["ctx_in"], 16)
                        pe.wait_ge(S["small_in"], 16 * 7)
                        pe.wait_ge(S["A_ok"], NG)
                    if k == 2:
                        pe.wait_ge(S["pre_ok"], 2)
                        pe.wait_ge(S["wq_ok"], 1)
                    if k == 3:
                        pe.wait_ge(S["bq_ok"], 1)
                    if i >= 2:
                        pe.wait_ge(S["pre_ok"], i - 1)
                    w, src = ((wkT_sb, ctxT_sb), (wvT_sb, ctxT_sb), (wq_sb, kpT), (bq_bc, kpT))[k]
                    mm(ps[:, MB[h], 0:HALF], w[:, :], src[:, h * HALF:(h + 1) * HALF],
                       start=True, stop=True).then_inc(S["pre_ps"], 1)
                elif 8 <= i < 10:
                    pe.wait_ge(S["pre_ok"], i - 1)
                    for j in range(4):
                        b = 4 * h + j
                        last = mm(ps[0:S2, MB[h], j * D:(j + 1) * D], vpT[:, b * S2:(b + 1) * S2], woT_sb[:, :],
                                  start=True, stop=True)
                    last.then_inc(S["vo_ps"], 1)
                elif i == 10:
                    pe.wait_ge(S["vo_ok"], 1)
                    pe.wait_ge(S["gate_in"], 32)
                    pe.wait_ge(S["consts_ok"], 2)
                    mm(ps[:, MB[0], 0:E], centre[:, :], gw_sb[:, :], start=True, stop=True) \
                        .then_inc(S["gw_ps"], 1)

            def chain(n, place):
                for b, k in chain_at(n, place, ("za", "z", "tr2", "sc2", "trp2", "o2", "tr3", "lg", "pf")):
                    chain_step(b, k)

            def chain_step(b, k):
                m = MB[b % 2]
                if k in ("za", "z"):
                    first = k == "za"
                    pe.wait_ge(S["y_ok"], 2 * b + (1 if first else 2))
                    if first:
                        pe.wait_ge(S["vo_ok"], 2)
                        pe.wait_ge(S["gw_ok"], 1)
                        if b >= 2:
                            pe.wait_ge(S["slot_ok"], b - 1)
                    for p in range(0 if first else NP // 2, NP // 2 if first else NP):
                        last = mm(ps[:, m, 0:D], yT_sb[:, b % 2, p, :], ww_sb[:, p, :],
                                  start=(p == 0), stop=(p == NP - 1))
                    last.then_inc(S["za_ps" if first else "z_ps"], 1)
                elif k == "tr2":
                    pe.wait_ge(S["x1_ok"], b + 1)
                    nc.tensor.transpose(ps[:, m, 0:T], x1[:, b % 2, :], ident[:, :]).then_inc(S["x1T_ps"], 1)
                elif k == "sc2":
                    pe.wait_ge(S["x1T_ok"], b + 1)
                    mm(ps[:, m, 0:S2], x1T[:, :], qk2[:, b * S2:(b + 1) * S2],
                       start=True, stop=True).then_inc(S["s2_ps"], 1)
                elif k == "trp2":
                    pe.wait_ge(S["p2_ok"], b + 1)
                    nc.tensor.transpose(ps[0:S2, m, 0:T], p2[:, :], ident[:, :]).then_inc(S["p2T_ps"], 1)
                elif k == "o2":
                    pe.wait_ge(S["p2T_ok"], b + 1)
                    mm(ps[:, m, 0:D], p2T[:, :], vo[:, b, :], start=True, stop=True).then_inc(S["o2_ps"], 1)
                elif k == "tr3":
                    pe.wait_ge(S["x2_ok"], b + 1)
                    nc.tensor.transpose(ps[:, m, 0:T], x2[:, b, :], ident[:, :]).then_inc(S["x2T_ps"], 1)
                elif k == "lg":
                    pe.wait_ge(S["x2T_ok"], b + 1)
                    mm(ps[:, m, 0:E], x2T[:, :], gw_centred[:, :], start=True, stop=True) \
                        .then_inc(S["lg_ps"], 1)
                elif k == "pf":
                    pe.wait_ge(S["oh_ok"], b + 1)
                    if b:
                        pe.wait_ge(S["taken_ok"], b)
                    mm(ps[:, m, 0:2 * E], before[:, :], oh[:, :, :].rearrange("p k e -> p (k e)"),
                       start=True, stop=False)
                    mm(ps[:, m, 0:2 * E], ones_b[:, :], taken[:, :, :].rearrange("p k e -> p (k e)"),
                       start=False, stop=True).then_inc(S["pf_ps"], 1)

            pe.wait_ge(S["consts_ok"], 1)
            for i in range(WARM[0]):
                mm(ps[:, SC[0], 0:P], ident[:, :], ident[:, :], start=True, stop=True)
            project(("x", 0))
            fold(0)
            fold(1)
            project(("t", 0))
            project(("t", 1))
            for n in STEPS:
                for it in ORDER["pe"]:
                    if it == "proj":
                        for u in projections(n):
                            project(u)
                    elif it == "scores" and 0 <= n + 1 < G:
                        scores(n + 1)
                    elif it == "trp" and 0 <= n - 1 < G:
                        transpose_p(n - 1)
                    elif it == "att" and 0 <= n - 2 < G:
                        attend(n - 2)
                    elif it[0] == "c":
                        chain(n, int(it[1]))
                        context(n, int(it[1]))

            def dispatch(e):
                pe.wait_ge(rows_in[e], 16)
                if e:
                    pe.wait_ge(S["dT_ok"], e)
                for i in range(NT):
                    last = nc.tensor.transpose(ps[:, DT, i * TILE:(i + 1) * TILE], dsp[0:TILE, e, i, 0:D],
                                               ident[0:TILE, 0:TILE])
                last.then_inc(S["dT_ps"], 1)

            def down(i):
                e, f = divmod(i, FC)
                pe.wait_ge(S["h_lo_ok"], i + 1)
                if f == 0 and e >= 2:
                    pe.wait_ge(S["oT_ok"], e - 1)
                cols = slice(f * D, (f + 1) * D)
                last = split_mm(ps[:, OT[e % 2], 0:SLOTS], w_hi[:, e % WR, 2, cols], w_lo[:, e % WR, 2, cols],
                                hT_hi[:, e % 2, f, :], hT_lo[:, e % 2, f, :],
                                start=(f == 0), stop=(f == FC - 1))
                if f == FC - 1:
                    last.then_inc(S["oT_ps"], 1)

            def by_row(e):
                pe.wait_ge(S["oT_ok"], e + 1)
                if e:
                    pe.wait_ge(S["eo_ok"], NT * e)
                for i in range(NT):
                    last = nc.tensor.transpose(ps[0:TILE, OUT_B, i * D:(i + 1) * D],
                                               oT[:, i * TILE:(i + 1) * TILE],
                                               ident[:, :])
                last.then_inc(S["o_ps"], 1)

            pe.wait_ge(S["w_hi_ok"], 3)
            for i in range(WARM[1]):
                mm(ps[:, PT, :], w_hi[:, 0, 0, 0:P], w_hi[:, 0, 0, :], start=True, stop=True)
            dispatch(0)
            for i in range(E * FC + FC_AFTER):
                e, f = divmod(i, FC)
                if e < E:
                    if f == 0:
                        pe.wait_ge(S["dT_ok"], e + 1)
                        pe.wait_ge(S["w_lo_ok"], 3 * (e + 1))
                    if i >= 2:
                        pe.wait_ge(S["h_ok"], i - 1)
                    cols = slice(f * P, (f + 1) * P)
                    split_mm(ps[:, GATE[i % 2], 0:SLOTS], w_hi[:, e % WR, 0, cols], w_lo[:, e % WR, 0, cols],
                             dT_hi[:, e % 2, :], dT_lo[:, e % 2, :]).then_inc(S["g_ps"], 1)
                    split_mm(ps[:, UP[i % 2], 0:SLOTS], w_hi[:, e % WR, 1, cols], w_lo[:, e % WR, 1, cols],
                             dT_hi[:, e % 2, :], dT_lo[:, e % 2, :]).then_inc(S["u_ps"], 1)
                expert_steps(2 * i, (("rows", dispatch), ("by_row", by_row)))
                if 0 <= i - DOWN_LAG < E * FC:
                    down(i - DOWN_LAG)
                expert_steps(2 * i + 1, (("rows", dispatch), ("by_row", by_row)))


def kernel(**inputs):
    import numpy as _np
    import concourse.bacc as _bacc
    from concourse import mybir as _mybir
    from concourse.bass_utils import run_bass_kernel_spmd as _run

    i = {k: _np.asarray(v) for k, v in inputs.items()}
    B, T, D = i["x"].shape
    DQ, _, H = i["L0_attn_Q"].shape
    DV = i["L0_attn_V"].shape[0]
    E, F, _ = i["L0_ffn_wi_gate"].shape

    def halves(w):
        return w.reshape(DQ, D, H // 8, 2, 4).transpose(3, 0, 2, 4, 1).reshape(2 * DQ, H // 2, D)

    arrays = {
        "x": i["x"],
        "ctxT": i["ctx_1024"].reshape(-1, D).T,
        "q_w": halves(i["L0_attn_Q"]),
        "k_w": halves(i["L0_attn_K"]),
        "v_w": i["L0_attn_V"].transpose(1, 2, 0).reshape(D, H * DV),
        "w_w": i["L0_attn_W"].reshape(D, DV, H // 2, 2).transpose(3, 1, 2, 0).reshape(2 * DV, H // 2, D),
        "wkT": i["L0_xattn_Wk"].T,
        "wvT": i["L0_xattn_Wv"].T,
        "bv": i["L0_xattn_bv"],
        "wq": i["L0_xattn_Wq"],
        "bq": i["L0_xattn_bq"],
        "woT": i["L0_xattn_Wo"].T,
        "bo": i["L0_xattn_bo"],
        "gate_wT": i["L0_ffn_gate_w"].T,
        "wgT": i["L0_ffn_wi_gate"].transpose(2, 0, 1),
        "wuT": i["L0_ffn_wi_up"].transpose(2, 0, 1),
        "wdT": i["L0_ffn_wo"].reshape(E, D, F // 128, 128).transpose(3, 0, 2, 1),
    }
    arrays = {k: _np.ascontiguousarray(v) for k, v in arrays.items()}
    nc = _bacc.Bacc("TRN2", target_bir_lowering=False, num_devices=1)
    args = [nc.dram_tensor(k, v.shape, _mybir.dt.from_np(v.dtype), kind="ExternalInput").ap()
            for k, v in arrays.items()]
    out = nc.dram_tensor("out", (B * T + SCRATCH_ROWS, D), _mybir.dt.float32, kind="ExternalOutput").ap()
    decoder_layer(nc, *args, out)
    r = _run(nc, [arrays], core_ids=[0])
    return r.results[0]["out"][:B * T].reshape(B, T, D)
```

```python
from contextlib import ExitStack

import concourse.bass as bass
from concourse import mybir

F32 = mybir.dt.float32
F32R = mybir.dt.float32r
BF16 = mybir.dt.bfloat16
I32 = mybir.dt.int32
U32 = mybir.dt.uint32
ALU = mybir.AluOpType
ACT = mybir.ActivationFunctionType
AX_X = mybir.AxisListType.X


SCRATCH_ROWS = 3 * 128


def decoder_layer(nc, x, ctxT, q_w, k_w, v_w, w_w, wkT, wvT, bv, wq, bq, woT, bo, gate_wT,
                  wgT, wuT, wdT, out):
    B, T, D = x.shape
    H = 2 * q_w.shape[1]
    DQ = q_w.shape[0] // 2
    DV = v_w.shape[1] // H
    S2 = ctxT.shape[1] // B
    E, F = wgT.shape[1:]
    N = B * T
    CAP = max(int(N / E * 1.25), 1)
    WR = 4
    NT = 3
    TILE = 2 * -(-CAP // NT)
    SLOTS = NT * TILE
    P = 128
    assert T == P and D == P and 2 * DV == P and 2 * DQ == P
    GH = 4
    NG = H // GH
    G = B * NG
    NP = H // 2
    FC = F // P
    assert E == 2 * WR and TILE <= P and NT * P == SCRATCH_ROWS
    ROW = D + 2
    EPS = 1e-5
    BIG = 1e30
    A_SCALE = -(DQ / D) / DQ
    Z_SCALE = (DV / D) ** 0.5 * (D / DV) ** 0.5 / H
    X_SCALE = -float(D) ** -0.5
    HALF = B * S2 // 2
    NV = 2
    VC = H * DV // NV
    TH = 2
    NJ = H // TH
    NTP = B // 2 * NJ
    TR = NJ + 2
    LEAD = 7

    disp = nc.dram_tensor("dispatched_rows", [E * SLOTS + 2 * B * P, ROW], F32).ap()

    with ExitStack() as ctx:
        def sb(name, shape, dt=F32):
            return ctx.enter_context(nc.sbuf_tensor(name, shape, dt))

        def sem(name):
            return ctx.enter_context(nc.semaphore(name))

        x2 = sb("x2", [P, B, D])
        bv_sb = sb("bv_sb", [P, 1])
        bq_sb = sb("bq_sb", [P, 1])
        gw_sb = sb("gw_sb", [P, E])
        gw_centred = sb("gw_centred", [P, E])
        w_raw = sb("w_raw", [P, 2, 3, F])
        w_first = [sb(f"w_{part}", [P, WR, 3, F], F32R) for part in ("hi", "lo")]

        ident = sb("ident", [P, P])
        before = sb("before", [P, P], BF16)
        ones_b = sb("ones_b", [P, P], BF16)
        iota_e = sb("iota_e", [P, 2, E])
        dump_row = sb("dump_row", [P, B, 2])
        base_row = sb("base_row", [P, B, 2])
        minus_one = sb("minus_one", [P, 1])
        minus_half = sb("minus_half", [P, B])
        blank = sb("blank", [P, NT, ROW])

        stat1 = sb("stat1", [P, B, 6])
        mv1 = sb("mv1", [P, B, 2])
        rstd1 = sb("rstd1", [P, B])
        smin = sb("smin", [P, 4, GH])
        ssum = sb("ssum", [P, 4, GH])
        sinv = sb("sinv", [P, 4, GH])

        stat = sb("stat", [P, 2, 6])
        mv = sb("mv", [P, 2, 2])
        rstd = sb("rstd", [P, 2])
        s2min = sb("s2min", [P, 1])
        s2sum = sb("s2sum", [P, 1])
        s2inv = sb("s2inv", [P, 1])
        rows = sb("rows", [P, 2, 2, ROW])
        x2T = sb("x2T", [P, T])
        diff = sb("diff", [P, 1])
        top8 = sb("top8", [P, 8])
        idx8 = sb("idx8", [P, 8], U32)
        idxf = sb("idxf", [P, 2])
        ratio = sb("ratio", [P, 1])
        denom = sb("denom", [P, 1])
        oh = sb("oh", [P, 2, E], BF16)
        taken = sb("taken", [P, 2, E], BF16)
        sbase = sb("sbase", [P, 2])
        prod = sb("prod", [P, 2, E])
        pos = sb("pos", [P, 2])
        rel = sb("rel", [P, 2])
        relok = sb("relok", [P, 2])
        slot = sb("slot", [P, B, 2], I32)

        with ExitStack() as attention_phase:
            def sb1(name, shape, dt=F32):
                return attention_phase.enter_context(nc.sbuf_tensor(name, shape, dt))

            A_hi = sb1("A_hi", [P, H, D], F32R)
            A_lo = sb1("A_lo", [P, H, D], F32R)
            t_hi = sb1("t_hi", [P, TR, TH, 2, T], F32R)
            t_lo = sb1("t_lo", [P, TR, TH, 2, T], F32R)
            with ExitStack() as weight_phase:
                def sb0(name, shape, dt=F32):
                    return weight_phase.enter_context(nc.sbuf_tensor(name, shape, dt))

                qw_sb = sb0("qw_sb", [P, H // 2, D])
                kw_sb = sb0("kw_sb", [P, H // 2, D])
            yT_sb = sb1("yT_sb", [P, 2, NP, T])
            x_sb = sb1("x_sb", [P, B, D])
            x1 = sb1("x1", [P, 2, D])
            ctxT_sb = sb1("ctxT_sb", [P, B * S2])
            vw_sb = sb1("vw_sb", [P, H * DV])
            ww_sb = sb1("ww_sb", [P, NP, D])
            wkT_sb = sb1("wkT_sb", [P, D])
            wvT_sb = sb1("wvT_sb", [P, D])
            wq_sb = sb1("wq_sb", [P, D])
            woT_sb = sb1("woT_sb", [P, D])
            bo_bc = sb1("bo_bc", [S2, D])
            vw_hi = sb1("vw_hi", [P, H * DV], F32R)
            vw_lo = sb1("vw_lo", [P, H * DV], F32R)
            xn = sb1("xn", [P, 2, D])
            xnT_hi = sb1("xnT_hi", [P, B, T], F32R)
            xnT_lo = sb1("xnT_lo", [P, B, T], F32R)
            kpT = sb1("kpT", [P, B * S2])
            vpT = sb1("vpT", [P, B * S2])
            qk2 = sb1("qk2", [P, B * S2])
            qbias = ctxT_sb
            bq_bc = sb1("bq_bc", [P, P])
            vo = sb1("vo", [S2, B, D])
            causal = sb1("causal", [P, P])
            x1T = bq_bc
            centre = sb1("centre", [P, D])
            wq_mean = sb1("wq_mean", [P, 1])
            s2_sb = sb1("s2_sb", [P, S2])
            p2 = sb1("p2", [P, S2])
            p2T = sb1("p2T", [S2, T])
            s_sb = sb1("s_sb", [P, 2, GH, T])
            v_sb = sb1("v_sb", [P, 2, H, DV])
            p_sb = sb1("p_sb", [P, 4, GH, T])
            pT_sb = sb1("pT_sb", [P, 2, GH, T])

        w_later = sb("w_later", [P, E - WR, 2, 3, F], F32R)
        dsp = sb("dsp", [P, E, NT, ROW])
        dT_hi = sb("dT_hi", [P, 2, SLOTS], F32R)
        dT_lo = sb("dT_lo", [P, 2, SLOTS], F32R)
        sg = sb("sg", [P, 2, SLOTS])
        hT = sb("hT", [P, 2, SLOTS])
        hT_hi = sb("hT_hi", [P, 2, FC, SLOTS], F32R)
        hT_lo = sb("hT_lo", [P, 2, FC, SLOTS], F32R)
        oT = sb("oT", [P, SLOTS])
        eo = sb("eo", [P, 2, NT, D])

        ps = ctx.enter_context(nc.psum_tensor("ps", [P, 8, 512], F32))
        PROJ, SC, PT, YB, MB = [0, 1], [2, 3], 4, 5, [6, 7]
        A_BANK = [PT, YB] + MB
        GATE, UP, DT, OT, OUT_B = [0, 1], [2, 3], 4, [5, 7], 6

        names = """vw_in ctx_in small_in gate_in consts_ok blank_ok blank_out
        mv1_ok rstd1_ok xn_ok xnT_lo_ok t_lo_ok A_ps A_hi_ok A_ok vw_hi_ok vw_lo_ok
        proj_ps proj_ok s_ps min_ok exp_ok sinv_ok pn_ok pt_ps pt_ok y_ps y_ok
        bq_ok wq_ok gw_ps gw_ok pre_ps pre_ok vo_ps vo_ok za_ps z_ps x1_ok mv2_ok mv3_ok rstd2_ok
        rstd3_ok s2_ok x1T_ps x1T_ok diff_ok s2_ps s2min_ok s2inv_ok p2_ok p2T_ps p2T_ok o2_ps x2_ok
        xn3_ok x2T_ps x2T_ok lg_ps
        top_ok ratio_ok wts_ok sbase_ok oh_ok pf_ps taken_ok slot_ok acc_out dve_step pool_step scattered
        w_hi_ok w_lo_ok dT_ps dT_hi_ok dT_ok g_ps u_ps sg_ok h_ok h_hi_ok h_lo_ok oT_ps oT_ok o_ps eo_ok
        added""".split()
        S = {n: sem(n) for n in names}
        qk_in = [sem(f"qk_in{i}") for i in range(2)]
        x_in = [sem(f"x_in{i}") for i in range(B // 2)]
        w_in = [sem(f"w_in{i}") for i in range(2)]
        rows_in = [sem(f"rows_in{e}") for e in range(E)]

        PLACE = dict(za=2, z=2, x1T=2, stat2=3, rstd2=3, tr2=3, sc2=6, min2=6, p2=6, trp2=9, p2T=9,
                     o2=12, stat3=12, x2T=12, tr3=13, rstd3=14, lg=15, choice=16, ratio=17, xn3=18,
                     pf=19, weights=19, slots=21, scatter=24)
        PREP = dict(stats=-4, rstd=-4, norm=-2, low=2)
        V_AT, V_FIRST = [-1, 0], [-1, 0]
        X_AT = {1: 1, 2: 6, 3: 14}
        T_FIRST = [2, 3, 1, 1, 1, 1, 2, 1, 1]
        PRE_FIRST = 11
        PT_ACT = (0, 1, 3)
        AT = dict(rows=-8, hi=-8, lo=-7, out=12, by_row=14, weigh=14)
        DOWN_LAG = 3
        FIRST_CHUNK, FIFTH_AT = 3, 26
        CHUNK_AT = {FIRST_CHUNK + i: i for i in range(3 * WR)}
        CHUNK_AT.update({FIFTH_AT + i: 3 * WR + i for i in range(3)})
        CHUNKS = 3 * WR + 3
        WARM = (8, 23)
        STEPS = range(-1, G + 3 + max(PLACE.values()) // 4)

        def chain_at(n, place, steps):
            at = 4 * n + place
            found = []
            for b in range(B):
                for k in steps:
                    if 4 * (NG * b + NG + 2) + PLACE[k] == at:
                        found.append((b, k))
            return found

        def projections(n):
            uses = []
            if n + 1 < len(T_FIRST):
                done = 2 + sum(T_FIRST[:n + 1])
                uses += [("t", t) for t in range(done, done + T_FIRST[n + 1])]
            elif n + LEAD < NTP:
                uses.append(("t", n + LEAD))
            for b in range(B):
                for k in range(NV):
                    if n == (NG * b + V_AT[k] if b else V_FIRST[k]):
                        uses.append(("v", b, k))
            uses += [("x", i) for i in X_AT if n == X_AT[i]]
            return uses

        def prepared(n, place, step):
            for i in X_AT:
                if 4 * (n - X_AT[i]) + place == PREP[step]:
                    return i

        USES = [("x", 0), ("t", 0), ("t", 1)] + [u for n in STEPS for u in projections(n)]
        TURN = {u: i for i, u in enumerate(USES)}

        PRE = {PRE_FIRST + i: i for i in range(11)}

        def expert_steps(at, steps):
            for name, step in steps:
                e, rest = divmod(at - AT[name], 2 * FC)
                if rest == 0 and 0 <= e < E and (e or AT[name] >= 0):
                    step(e)

        def split_w(part, e, k):
            return w_first[part][:, e, k, :] if e < WR else w_later[:, e - WR, part, k, :]

        block = ctx.enter_context(nc.Block())

        @block.sync
        def _(sp):
            def load_x(i):
                sp.dma_start(x_sb[:, 2 * i:2 * i + 2, :], x[2 * i:2 * i + 2].rearrange("b t d -> t b d")) \
                    .then_inc(x_in[i], 16)

            load_x(0)
            for i in range(2):
                half = slice(i * NP // 2, (i + 1) * NP // 2)
                sp.dma_start(kw_sb[:, half, :], k_w[:, half, :]).then_inc(qk_in[i], 16)
            sp.dma_start(vw_sb[:, :], v_w).then_inc(S["vw_in"], 16)
            load_x(1)
            sp.dma_start(ctxT_sb[:, :], ctxT).then_inc(S["ctx_in"], 16)
            for dst, src in ((wkT_sb, wkT), (wvT_sb, wvT), (wq_sb, wq), (woT_sb, woT),
                             (bv_sb, bv.rearrange("(p a) -> p a", a=1)),
                             (bq_sb, bq.rearrange("(p a) -> p a", a=1)),
                             (bo_bc, bo.rearrange("(a d) -> a d", a=1).to_broadcast([S2, D]))):
                sp.dma_start(dst[:, :], src).then_inc(S["small_in"], 16)
            sp.dma_start(ww_sb[:, :, :], w_w).then_inc(S["gate_in"], 16)
            sp.dma_start(gw_sb[:, :], gate_wT).then_inc(S["gate_in"], 16)
            load_x(2)
            load_x(3)

            def load_expert(e):
                if e >= 2:
                    sp.wait_ge(S["w_hi_ok"], 3 * (e - 1))
                    sp.wait_ge(S["w_lo_ok"], 3 * (e - 1))
                sp.dma_start(w_raw[:, e % 2, 0, :], wgT[:, e, :]).then_inc(w_in[e % 2], 16)
                sp.dma_start(w_raw[:, e % 2, 1, :], wuT[:, e, :]).then_inc(w_in[e % 2], 16)
                sp.dma_start(w_raw[:, e % 2, 2, :], wdT[:, e, :, :].rearrange("p f d -> p (f d)")) \
                    .then_inc(w_in[e % 2], 16)

            load_expert(0)
            load_expert(1)
            sp.wait_ge(S["blank_ok"], 2)
            rows_of = disp[0:E * SLOTS, :].rearrange("(e s) r -> s e r", e=E)
            for i in range(NT):
                sp.dma_start(rows_of[i * TILE:(i + 1) * TILE],
                             blank[0:TILE, i, :].unsqueeze(1).to_broadcast([TILE, E, ROW])) \
                    .then_inc(S["blank_out"], 16)
            sp.dma_start(out[N:N + NT * P, :].rearrange("(t p) d -> p t d", p=P), blank[:, :, 0:D]) \
                .then_inc(S["blank_out"], 16)
            for b in range(B):
                if b + 2 < WR + 2:
                    load_expert(b + 2)
                if b == B - 1:
                    load_expert(WR + 2)
                sp.wait_ge(S["x2_ok"], b + 1)
                sp.dma_start(out[b * T:(b + 1) * T, :], x2[:, b, :]).then_inc(S["acc_out"], 16)
            sp.wait_ge(S["scattered"], 2 * B * 16)
            for e in range(E):
                sp.dma_start(dsp[0:TILE, e, :, :],
                             disp[e * SLOTS:(e + 1) * SLOTS, :].rearrange("(p t) r -> p t r", t=NT)) \
                    .then_inc(rows_in[e], 16)
            load_expert(E - 1)
            sp.wait_ge(S["added"], 16 * NT * E)

        @block.gpsimd
        def _(pool):
            g = nc.gpsimd
            n_link = [0]

            def link(ins):
                n_link[0] += 1
                ins.then_inc(S["pool_step"], 1)
                pool.wait_ge(S["pool_step"], n_link[0])

            g.memset(minus_half[:, :], -0.5)
            g.memset(minus_one[:, :], -1.0)
            link(g.memset(ident[:, :], 0.0))
            g.affine_select(out=ident[:, :], in_=ident[:, :], compare_op=ALU.not_equal, fill=1.0,
                            base=0, pattern=[[-1, P]], channel_multiplier=1)
            link(g.memset(causal[:, :], 0.0))
            g.affine_select(out=causal[:, :], in_=causal[:, :], compare_op=ALU.is_ge, fill=BIG,
                            base=0, pattern=[[-1, P]], channel_multiplier=1).then_inc(S["consts_ok"], 1)

            def rstd_1(i):
                pool.wait_ge(S["mv1_ok"], i + 1)
                two = rstd1[:, 2 * i:2 * i + 2]
                link(g.tensor_scalar(two, mv1[:, 2 * i:2 * i + 2, 1], EPS, None, ALU.add))
                g.tensor_tensor(two, two, minus_half[:, 0:2], ALU.pow).then_inc(S["rstd1_ok"], 1)

            rstd_1(0)
            g.tensor_scalar(centre[:, :], ident[:, :], -1.0 / D, None, ALU.add).then_inc(S["consts_ok"], 1)
            for i in range(NV):
                pool.wait_ge(S["vw_hi_ok"], i + 1)
                cols = slice(i * VC, (i + 1) * VC)
                g.tensor_tensor(vw_lo[:, cols], vw_sb[:, cols], vw_hi[:, cols].bitcast(F32), ALU.subtract) \
                    .then_inc(S["vw_lo_ok"], 1)
            link(g.memset(before[:, :], 1.0))
            g.affine_select(out=before[:, :], in_=before[:, :], compare_op=ALU.is_ge, fill=0.0,
                            base=-1, pattern=[[1, P]], channel_multiplier=-1)
            g.memset(ones_b[:, :], 1.0)
            g.iota(iota_e[:, :, :], pattern=[[0, 2], [1, E]], base=0, channel_multiplier=0,
                   allow_small_or_imprecise_dtypes=True)
            g.iota(dump_row[:, :, :], pattern=[[2 * P, B], [P, 2]], base=E * SLOTS, channel_multiplier=1,
                   allow_small_or_imprecise_dtypes=True)
            g.iota(base_row[:, :, :], pattern=[[-2 * P, B], [CAP - P, 2]], base=-E * SLOTS,
                   channel_multiplier=-1, allow_small_or_imprecise_dtypes=True)
            g.memset(taken[:, :, :], 0.0)
            g.memset(blank[:, :, 0:D + 1], 0.0).then_inc(S["blank_ok"], 1)
            g.iota(blank[:, :, D + 1].bitcast(I32), pattern=[[P, NT]], base=N,
                   channel_multiplier=1).then_inc(S["blank_ok"], 1)
            def split_lo(i):
                e, k = divmod(i, 3)
                pool.wait_ge(S["w_hi_ok"], i + 1)
                g.tensor_tensor(split_w(1, e, k), w_raw[:, e % 2, k, :], split_w(0, e, k).bitcast(F32),
                                ALU.subtract).then_inc(S["w_lo_ok"], 1)

            def rstd_of(k, b):
                pool.wait_ge(S[f"mv{2 + k}_ok"], b + 1)
                if k and b:
                    pool.wait_ge(S["ratio_ok"], b)
                one = rstd[:, k:k + 1]
                link(g.tensor_scalar(one, mv[:, k, 1:2], EPS, None, ALU.add))
                g.tensor_tensor(one, one, minus_half[:, 0:1], ALU.pow).then_inc(S[f"rstd{2 + k}_ok"], 1)

            def chain(n, place):
                i = prepared(n, place, "rstd")
                if i is not None:
                    rstd_1(i)
                for b, k in chain_at(n, place, ("rstd2", "rstd3", "weights", "scatter")):
                    if k == "rstd2":
                        rstd_of(0, b)
                    elif k == "rstd3":
                        rstd_of(1, b)
                    elif k == "weights":
                        pool.wait_ge(S["ratio_ok"], b + 1)
                        if b:
                            pool.wait_ge(S["scattered"], 2 * b * 16)
                        link(g.tensor_scalar(denom[:, :], ratio[:, :], 1.0, None, ALU.add))
                        link(g.tensor_tensor(rows[:, b % 2, 0, D:D + 1], denom[:, :], minus_one[:, :], ALU.pow))
                        g.tensor_tensor(rows[:, b % 2, 1, D:D + 1], ratio[:, :], rows[:, b % 2, 0, D:D + 1],
                                        ALU.mult).then_inc(S["wts_ok"], 1)
                    else:
                        if b == 0:
                            pool.wait_ge(S["blank_out"], 16 * 4)
                        if b:
                            pool.wait_ge(S["scattered"], 2 * b * 16)
                        link(g.iota(rows[:, b % 2, :, D + 1].bitcast(I32), pattern=[[0, 2]], base=b * T,
                                    channel_multiplier=1))
                        pool.wait_ge(S["slot_ok"], b + 1)
                        pool.wait_ge(S["wts_ok"], b + 1)
                        for c in range(2):
                            pool.indirect_dma_start(
                                out=disp, out_offset=bass.IndirectOffsetOnAxis(ap=slot[:, b, c:c + 1], axis=0),
                                in_=rows[:, b % 2, c, :], in_offset=None).then_inc(S["scattered"], 16)

            for n in STEPS:
                chain(n, 0)
                if 0 <= n < G:
                    pool.wait_ge(S["sinv_ok"], n + 1)
                    g.tensor_tensor(p_sb[:, n % 4, :, :], p_sb[:, n % 4, :, :],
                                    sinv[:, n % 4, :].unsqueeze(2).to_broadcast([P, GH, T]), ALU.mult) \
                        .then_inc(S["pn_ok"], 1)
                chain(n, 1)
                if n in CHUNK_AT:
                    split_lo(CHUNK_AT[n])
                chain(n, 2)
                chain(n, 3)

            for i in range(CHUNKS, 3 * E):
                split_lo(i)
            pool.wait_ge(S["acc_out"], 16 * B)
            for e in range(E):
                pool.wait_ge(S["eo_ok"], NT * (e + 1))
                if e:
                    pool.wait_ge(S["added"], 16 * NT * e)
                for i in range(NT):
                    pool.indirect_dma_start(
                        out=out, out_offset=bass.IndirectOffsetOnAxis(
                            ap=dsp[0:TILE, e, i, D + 1:D + 2].bitcast(I32), axis=0),
                        in_=eo[0:TILE, e % 2, i, :], in_offset=None, compute_op=ALU.add) \
                        .then_inc(S["added"], 16)

        @block.scalar
        def _(act):
            a = nc.scalar
            for i in range(2):
                half = slice(i * NP // 2, (i + 1) * NP // 2)
                act.dma_start(qw_sb[:, half, :], q_w[:, half, :]).then_inc(qk_in[i], 16)

            def high_A(i):
                act.wait_ge(S["A_ps"], 2 * (i // 2 + 1))
                a.activation(A_hi[:, GH * i:GH * i + GH, :], ps[:, A_BANK[i], :], ACT.Copy,
                             scale=A_SCALE).then_inc(S["A_hi_ok"], 1)

            def copy_projection(u):
                act.wait_ge(S["proj_ps"], TURN[u] + 1)
                src = ps[:, PROJ[TURN[u] % 2], :]
                if u[0] == "x":
                    a.copy(xnT_hi[:, 2 * u[1]:2 * u[1] + 2, :], src[:, 0:2 * T]).then_inc(S["proj_ok"], 1)
                    return
                if u[0] == "t":
                    if u[1] >= TR:
                        p, j = divmod(u[1] - TR, NJ)
                        act.wait_ge(S["s_ps"], NG * (2 * p + 1) + TH * j // GH + 1)
                    dst = t_hi[:, u[1] % TR, :, :, :]
                else:
                    _, b, i = u
                    if b >= 2:
                        act.wait_ge(S["y_ps"], NG * (b - 1))
                    dst = v_sb[:, b % 2, i * (H // NV):(i + 1) * (H // NV), :]
                a.copy(dst, src).then_inc(S["proj_ok"], 1)

            def copy_y(i):
                b, k = divmod(i, 2)
                act.wait_ge(S["y_ps"], 2 * i + 2)
                if b >= 2:
                    act.wait_ge(S["z_ps"], b - 1)
                a.copy(yT_sb[:, b % 2, 4 * k:4 * k + 4, :], ps[:, YB, :]).then_inc(S["y_ok"], 1)

            def copy_pt(n):
                act.wait_ge(S["pt_ps"], n + 1)
                if n >= 2:
                    act.wait_ge(S["y_ps"], n - 1)
                a.copy(pT_sb[:, n % 2, :, :], ps[:, PT, :]).then_inc(S["pt_ok"], 1)

            def exps(n):
                act.wait_ge(S["min_ok"], n + 1)
                if n >= 4:
                    act.wait_ge(S["pt_ps"], n - 3)
                    act.wait_ge(S["sinv_ok"], n - 3)
                for h in range(GH):
                    last = a.activation(p_sb[:, n % 4, h, :], s_sb[:, n % 2, h, :], ACT.Exp,
                                        bias=smin[:, n % 4, h:h + 1], scale=-1.0,
                                        accum_out=ssum[:, n % 4, h:h + 1])
                last.then_inc(S["exp_ok"], 1)

            def chain(n, place):
                for b, k in chain_at(n, place, ("x1T", "p2", "p2T", "x2T", "ratio")):
                    m = MB[b % 2]
                    if k == "x1T":
                        act.wait_ge(S["x1T_ps"], b + 1)
                        a.copy(x1T[:, :], ps[:, m, 0:T]).then_inc(S["x1T_ok"], 1)
                    elif k == "p2":
                        act.wait_ge(S["s2min_ok"], b + 1)
                        a.activation(p2[:, :], s2_sb[:, :], ACT.Exp, bias=s2min[:, :], scale=-1.0,
                                     accum_out=s2sum[:, :]).then_inc(S["p2_ok"], 1)
                    elif k == "p2T":
                        act.wait_ge(S["p2T_ps"], b + 1)
                        a.copy(p2T[:, :], ps[0:S2, m, 0:T]).then_inc(S["p2T_ok"], 1)
                    elif k == "x2T":
                        act.wait_ge(S["x2T_ps"], b + 1)
                        a.copy(x2T[:, :], ps[:, m, 0:T]).then_inc(S["x2T_ok"], 1)
                    else:
                        act.wait_ge(S["diff_ok"], b + 1)
                        act.wait_ge(S["rstd3_ok"], b + 1)
                        if b:
                            act.wait_ge(S["wts_ok"], b)
                        a.activation(ratio[:, :], diff[:, :], ACT.Exp, scale=rstd[:, 1:2]) \
                            .then_inc(S["ratio_ok"], 1)

            copy_projection(("x", 0))
            act.wait_ge(S["vw_in"], 16)
            for i in range(NV):
                a.copy(vw_hi[:, i * VC:(i + 1) * VC], vw_sb[:, i * VC:(i + 1) * VC]).then_inc(S["vw_hi_ok"], 1)
            high_A(0)
            high_A(1)
            copy_projection(("t", 0))
            copy_projection(("t", 1))
            high_A(2)
            high_A(3)
            for n in STEPS:
                for u in projections(n):
                    copy_projection(u)
                chain(n, 0)
                chain(n, 1)
                if 0 <= n - 1 < G and (n - 1) % 4 in PT_ACT:
                    copy_pt(n - 1)
                if 0 <= n + 1 < G:
                    exps(n + 1)
                chain(n, 2)
                chain(n, 3)
                if 0 <= n - 2 < G and n % 2:
                    copy_y((n - 2) // 2)

            def dispatch_hi(e):
                act.wait_ge(S["dT_ps"], e + 1)
                if e >= 2:
                    act.wait_ge(S["u_ps"], FC * (e - 1))
                a.copy(dT_hi[:, e % 2, :], ps[:, DT, 0:SLOTS]).then_inc(S["dT_hi_ok"], 1)

            def out_of(e):
                act.wait_ge(S["oT_ps"], e + 1)
                if e:
                    act.wait_ge(S["o_ps"], e)
                a.copy(oT[:, :], ps[:, OT[e % 2], 0:SLOTS]).then_inc(S["oT_ok"], 1)

            def weigh(e):
                act.wait_ge(S["o_ps"], e + 1)
                if e >= 2:
                    act.wait_ge(S["added"], 16 * NT * (e - 1))
                for i in range(NT):
                    a.activation(eo[0:TILE, e % 2, i, :], ps[0:TILE, OUT_B, i * D:(i + 1) * D],
                                 ACT.Copy, scale=dsp[0:TILE, e, i, D:D + 1]).then_inc(S["eo_ok"], 1)

            dispatch_hi(0)
            for i in range((E + 2) * FC):
                e, f = divmod(i, FC)
                if e < E:
                    act.wait_ge(S["g_ps"], i + 1)
                    if i >= 2:
                        act.wait_ge(S["h_ok"], i - 1)
                    a.activation(sg[:, i % 2, :], ps[:, GATE[i % 2], 0:SLOTS], ACT.Silu) \
                        .then_inc(S["sg_ok"], 1)
                expert_steps(2 * i, (("hi", dispatch_hi), ("out", out_of), ("weigh", weigh)))
                if e < E:
                    act.wait_ge(S["h_ok"], i + 1)
                    if e >= 2:
                        act.wait_ge(S["oT_ps"], e - 1)
                    a.copy(hT_hi[:, e % 2, f, :], hT[:, i % 2, :]).then_inc(S["h_hi_ok"], 1)
                expert_steps(2 * i + 1, (("hi", dispatch_hi), ("out", out_of), ("weigh", weigh)))

        @block.vector
        def _(dve):
            v = nc.vector
            n_link = [0]

            def link(ins):
                n_link[0] += 1
                ins.then_inc(S["dve_step"], 1)
                dve.wait_ge(S["dve_step"], n_link[0])

            def layer_norm_1(i):
                dve.wait_ge(x_in[i], 16)
                for b in (2 * i, 2 * i + 1):
                    ins = v.bn_stats(stat1[:, b, :], x_sb[:, b, :])
                link(ins)
                for b in (2 * i, 2 * i + 1):
                    last = v.bn_aggr(mv1[:, b, :], stat1[:, b, :])
                last.then_inc(S["mv1_ok"], 1)

            def normed_1(i):
                dve.wait_ge(S["rstd1_ok"], i + 1)
                dve.wait_ge(S["mv1_ok"], i + 1)
                if i:
                    dve.wait_ge(S["proj_ps"], TURN["x", i - 1] + 1)
                for b in (2 * i, 2 * i + 1):
                    last = v.tensor_scalar(xn[:, b % 2, :], x_sb[:, b, :], mv1[:, b, 0:1], rstd1[:, b:b + 1],
                                           ALU.subtract, ALU.mult)
                last.then_inc(S["xn_ok"], 1)

            def transposed_1(i):
                dve.wait_ge(S["proj_ok"], TURN["x", i] + 1)
                src = ps[:, PROJ[TURN["x", i] % 2], 0:2 * T]
                two = xnT_hi[:, 2 * i:2 * i + 2, :].bitcast(F32).rearrange("p b t -> p (b t)")
                v.tensor_tensor(xnT_lo[:, 2 * i:2 * i + 2, :].rearrange("p b t -> p (b t)"), src, two,
                                ALU.subtract).then_inc(S["xnT_lo_ok"], 1)

            def low_t(t):
                turn = TURN["t", t]
                dve.wait_ge(S["proj_ok"], turn + 1)
                if t >= TR:
                    p, j = divmod(t - TR, NJ)
                    dve.wait_ge(S["s_ps"], NG * (2 * p + 1) + TH * j // GH + 1)
                parts = [x[:, t % TR, :, :, :].rearrange("p h b t -> p (h b t)") for x in (t_lo, t_hi)]
                v.tensor_tensor(parts[0], ps[:, PROJ[turn % 2], :], parts[1].bitcast(F32), ALU.subtract) \
                    .then_inc(S["t_lo_ok"], 1)

            def low_A(i):
                dve.wait_ge(S["A_hi_ok"], i + 1)
                v.scalar_tensor_tensor(out=A_lo[:, GH * i:GH * i + GH, :].rearrange("p h d -> p (h d)"),
                                       in0=ps[:, A_BANK[i], :], scalar=A_SCALE,
                                       in1=A_hi[:, GH * i:GH * i + GH, :].bitcast(F32)
                                       .rearrange("p h d -> p (h d)"),
                                       op0=ALU.mult, op1=ALU.subtract).then_inc(S["A_ok"], 1)

            layer_norm_1(0)
            normed_1(0)
            transposed_1(0)
            low_A(0)
            low_A(1)
            low_t(0)
            low_t(1)
            low_A(2)
            low_A(3)

            def row_min(n):
                dve.wait_ge(S["s_ps"], n + 1)
                if n >= 2:
                    dve.wait_ge(S["exp_ok"], n - 1)
                for h in range(GH):
                    last = v.tensor_tensor_reduce(out=s_sb[:, n % 2, h, :], in0=ps[:, SC[n % 2], h * T:(h + 1) * T],
                                                  in1=causal[:, :], scale=1.0, scalar=3e38,
                                                  op0=ALU.add, op1=ALU.min, accum_out=smin[:, n % 4, h:h + 1])
                last.then_inc(S["min_ok"], 1)

            def inverse(n):
                dve.wait_ge(S["exp_ok"], n + 1)
                if n >= 4:
                    dve.wait_ge(S["pn_ok"], n - 3)
                v.reciprocal(sinv[:, n % 4, :], ssum[:, n % 4, :]).then_inc(S["sinv_ok"], 1)

            def copy_pt(n):
                dve.wait_ge(S["pt_ps"], n + 1)
                if n >= 2:
                    dve.wait_ge(S["y_ps"], n - 1)
                v.tensor_copy(pT_sb[:, n % 2, :, :], ps[:, PT, :]).then_inc(S["pt_ok"], 1)

            def pre_copy(i):
                dve.wait_ge(S["pre_ps"], i + 1)
                k, h = divmod(i, 2)
                cols = slice(h * HALF, (h + 1) * HALF)
                src = ps[:, MB[i % 2], 0:HALF]
                if k == 0:
                    ins = v.tensor_scalar(kpT[:, cols], src, X_SCALE, None, ALU.mult)
                elif k == 1:
                    ins = v.tensor_scalar(vpT[:, cols], src, bv_sb[:, 0:1], None, ALU.add)
                elif k == 2:
                    ins = v.tensor_copy(qk2[:, cols], src)
                else:
                    ins = v.tensor_copy(qbias[:, cols], src)
                ins.then_inc(S["pre_ok"], 1)

            def pre_vo(i):
                dve.wait_ge(S["vo_ps"], i + 1)
                v.tensor_tensor(vo[:, 4 * i:4 * i + 4, :], ps[0:S2, MB[i], :].rearrange("p (b d) -> p b d", b=4),
                                bo_bc[:, :].unsqueeze(1).to_broadcast([S2, 4, D]), ALU.add) \
                    .then_inc(S["vo_ok"], 1)

            def stats(k, src):
                link(v.bn_stats(stat[:, k, :], src))
                v.bn_aggr(mv[:, k, :], stat[:, k, :]).then_inc(S[f"mv{2 + k}_ok"], 1)

            def chain(n, place):
                for k, step in (("stats", layer_norm_1), ("norm", normed_1), ("low", transposed_1)):
                    i = prepared(n, place, k)
                    if i is not None:
                        step(i)
                for b, k in chain_at(n, place, ("stat2", "min2", "trp2", "stat3", "xn3", "choice",
                                                "weights", "slots")):
                    chain_step(b, k)

            def chain_step(b, k):
                m = MB[b % 2]
                if k == "stat2":
                    dve.wait_ge(S["z_ps"], b + 1)
                    v.scalar_tensor_tensor(out=x1[:, b % 2, :], in0=ps[:, m, 0:D], scalar=Z_SCALE,
                                           in1=x_sb[:, b, :], op0=ALU.mult, op1=ALU.add) \
                        .then_inc(S["x1_ok"], 1)
                    dve.wait_ge(S["x1_ok"], b + 1)
                    stats(0, x1[:, b % 2, :])
                elif k == "min2":
                    dve.wait_ge(S["s2_ps"], b + 1)
                    if b:
                        dve.wait_ge(S["p2_ok"], b)
                    dve.wait_ge(S["rstd2_ok"], b + 1)
                    v.scalar_tensor_tensor(out=s2_sb[:, :], in0=ps[:, m, 0:S2], scalar=rstd[:, 0:1],
                                           in1=qbias[:, b * S2:(b + 1) * S2], op0=ALU.mult, op1=ALU.add) \
                        .then_inc(S["s2_ok"], 1)
                    dve.wait_ge(S["s2_ok"], b + 1)
                    v.tensor_reduce(s2min[:, :], s2_sb[:, :], axis=AX_X, op=ALU.min) \
                        .then_inc(S["s2min_ok"], 1)
                elif k == "trp2":
                    dve.wait_ge(S["p2_ok"], b + 1)
                    v.reciprocal(s2inv[:, :], s2sum[:, :]).then_inc(S["s2inv_ok"], 1)
                elif k == "stat3":
                    dve.wait_ge(S["o2_ps"], b + 1)
                    dve.wait_ge(S["s2inv_ok"], b + 1)
                    v.scalar_tensor_tensor(out=x2[:, b, :], in0=ps[:, m, 0:D], scalar=s2inv[:, 0:1],
                                           in1=x1[:, b % 2, :], op0=ALU.mult, op1=ALU.add) \
                        .then_inc(S["x2_ok"], 1)
                    dve.wait_ge(S["x2_ok"], b + 1)
                    stats(1, x2[:, b, :])
                elif k == "xn3":
                    dve.wait_ge(S["rstd3_ok"], b + 1)
                    if b >= 2:
                        dve.wait_ge(S["scattered"], 2 * b * 16)
                    v.tensor_scalar(rows[:, b % 2, :, 0:D], x2[:, b, :].unsqueeze(1).to_broadcast([P, 2, D]),
                                    mv[:, 1, 0:1], rstd[:, 1:2], ALU.subtract, ALU.mult) \
                        .then_inc(S["xn3_ok"], 1)
                elif k == "choice":
                    dve.wait_ge(S["lg_ps"], b + 1)
                    if b:
                        dve.wait_ge(S["ratio_ok"], b)
                    v.max(top8[:, :], ps[:, m, 0:E]).then_inc(S["top_ok"], 1)
                    dve.wait_ge(S["top_ok"], b + 1)
                    v.tensor_tensor(diff[:, :], top8[:, 1:2], top8[:, 0:1], ALU.subtract) \
                        .then_inc(S["diff_ok"], 1)
                    link(v.max_index(idx8[:, :], top8[:, :], ps[:, m, 0:E]))
                    link(v.tensor_copy(idxf[:, :], idx8[:, 0:2]))
                    v.tensor_tensor(oh[:, :, :], iota_e[:, :, :], idxf[:, :].unsqueeze(2).to_broadcast([P, 2, E]),
                                    ALU.is_equal).then_inc(S["oh_ok"], 1)
                elif k == "weights":
                    v.scalar_tensor_tensor(out=sbase[:, :], in0=idxf[:, :], scalar=float(SLOTS),
                                           in1=base_row[:, b, :], op0=ALU.mult, op1=ALU.add) \
                        .then_inc(S["sbase_ok"], 1)
                elif k == "slots":
                    dve.wait_ge(S["pf_ps"], b + 1)
                    dve.wait_ge(S["oh_ok"], b + 1)
                    link(v.tensor_tensor(prod[:, :, :], ps[:, m, 0:2 * E].rearrange("p (k e) -> p k e", k=2),
                                         oh[:, :, :], ALU.mult))
                    v.tensor_tensor(taken[:, :, :], taken[:, :, :], oh[:, :, :], ALU.add) \
                        .then_inc(S["taken_ok"], 1)
                    link(v.tensor_reduce(pos[:, :], prod[:, :, :], axis=AX_X, op=ALU.add))
                    dve.wait_ge(S["sbase_ok"], b + 1)
                    link(v.tensor_tensor(rel[:, :], pos[:, :], sbase[:, :], ALU.add))
                    link(v.scalar_tensor_tensor(out=relok[:, :], in0=pos[:, :], scalar=float(CAP),
                                                in1=rel[:, :], op0=ALU.is_lt, op1=ALU.mult))
                    v.tensor_tensor(slot[:, b, :], relok[:, :], dump_row[:, b, :], ALU.add) \
                        .then_inc(S["slot_ok"], 1)

            def split_hi(i):
                e, k = divmod(i, 3)
                dve.wait_ge(w_in[e % 2], 48 * (e // 2 + 1))
                if i == 3 * WR:
                    dve.wait_ge(S["proj_ps"], TURN["t", NTP - 1] + 1)
                if i == 3 * (WR + 1):
                    dve.wait_ge(S["s_ps"], G)
                v.tensor_copy(split_w(0, e, k), w_raw[:, e % 2, k, :]).then_inc(S["w_hi_ok"], 1)

            def context(n, place):
                i = PRE.get(4 * n + place, -1)
                if i == 0:
                    dve.wait_ge(S["small_in"], 16 * 7)
                    link(v.tensor_reduce(wq_mean[:, :], wq_sb[:, :], axis=AX_X, op=ALU.add))
                    link(v.tensor_scalar(wq_mean[:, :], wq_mean[:, :], 1.0 / D, None, ALU.mult))
                    v.tensor_scalar(wq_sb[:, :], wq_sb[:, :], wq_mean[:, 0:1], None, ALU.subtract) \
                        .then_inc(S["wq_ok"], 1)
                    v.tensor_copy(bq_bc[:, :], bq_sb[:, 0:1].to_broadcast([P, P])).then_inc(S["bq_ok"], 1)
                if 0 <= i < 8:
                    pre_copy(i)
                elif 8 <= i < 10:
                    pre_vo(i - 8)
                elif i == 10:
                    dve.wait_ge(S["gw_ps"], 1)
                    v.tensor_copy(gw_centred[:, :], ps[:, MB[0], 0:E]).then_inc(S["gw_ok"], 1)

            for n in STEPS:
                if n + 1 in CHUNK_AT:
                    split_hi(CHUNK_AT[n + 1])
                chain(n, 0)
                context(n, 0)
                if 0 <= n + 1 < G:
                    row_min(n + 1)
                if 0 <= n < G:
                    inverse(n)
                chain(n, 1)
                context(n, 1)
                for u in projections(n):
                    if u[0] == "t":
                        low_t(u[1])
                chain(n, 2)
                context(n, 2)
                if 0 <= n - 1 < G and (n - 1) % 4 not in PT_ACT:
                    copy_pt(n - 1)
                chain(n, 3)
                context(n, 3)

            def dispatch_lo(e):
                dve.wait_ge(S["dT_hi_ok"], e + 1)
                v.tensor_tensor(dT_lo[:, e % 2, :], ps[:, DT, 0:SLOTS], dT_hi[:, e % 2, :].bitcast(F32),
                                ALU.subtract).then_inc(S["dT_ok"], 1)

            def hidden_lo(i):
                e, f = divmod(i, FC)
                dve.wait_ge(S["h_hi_ok"], i + 1)
                v.tensor_tensor(hT_lo[:, e % 2, f, :], hT[:, i % 2, :], hT_hi[:, e % 2, f, :].bitcast(F32),
                                ALU.subtract).then_inc(S["h_lo_ok"], 1)

            for i in range(CHUNKS, 3 * (E - 1)):
                split_hi(i)
            dispatch_lo(0)
            for i in range(E * FC + 1):
                if i < E * FC:
                    dve.wait_ge(S["sg_ok"], i + 1)
                    dve.wait_ge(S["u_ps"], i + 1)
                    if i >= 2:
                        dve.wait_ge(S["h_lo_ok"], i - 1)
                    v.tensor_tensor(hT[:, i % 2, :], ps[:, UP[i % 2], 0:SLOTS], sg[:, i % 2, :], ALU.mult) \
                        .then_inc(S["h_ok"], 1)
                expert_steps(2 * i, (("lo", dispatch_lo),))
                if i:
                    hidden_lo(i - 1)
                expert_steps(2 * i + 1, (("lo", dispatch_lo),))
                if 1 <= i <= 3:
                    split_hi(3 * (E - 1) + i - 1)

        @block.tensor
        def _(pe):
            mm = nc.tensor.matmul
            def fold(c):
                pe.wait_ge(qk_in[c], 32)
                for j in range(GH):
                    for r in range(2):
                        k = GH * c + j
                        ins = mm(ps[:, A_BANK[2 * c + r], j * D:(j + 1) * D], kw_sb[r * DQ:(r + 1) * DQ, k, :],
                                 qw_sb[r * DQ:(r + 1) * DQ, k, :], start=True, stop=True)
                        if j == GH - 1:
                            ins.then_inc(S["A_ps"], 1)

            def split_mm(out_ap, w_hi_ap, w_lo_ap, m_hi_ap, m_lo_ap, start=True, stop=True):
                mm(out_ap, w_hi_ap, m_lo_ap, start=start, stop=False)
                mm(out_ap, w_hi_ap, m_hi_ap, start=False, stop=False)
                return mm(out_ap, w_lo_ap, m_hi_ap, start=False, stop=stop)

            def project(u):
                turn = TURN[u]
                if turn >= 2:
                    pe.wait_ge(S["proj_ok"], turn - 1)
                    had = USES[turn - 2]
                    if had[0] == "x":
                        pe.wait_ge(S["xnT_lo_ok"], had[1] + 1)
                    elif had[0] == "t":
                        pe.wait_ge(S["t_lo_ok"], had[1] + 1)
                bank = ps[:, PROJ[turn % 2], :]
                if u[0] == "x":
                    pe.wait_ge(S["consts_ok"], 1)
                    pe.wait_ge(S["xn_ok"], u[1] + 1)
                    for j in range(2):
                        last = nc.tensor.transpose(bank[:, j * T:(j + 1) * T], xn[:, j, :],
                                                   ident[:, :])
                    last.then_inc(S["proj_ps"], 1)
                    return
                if u[0] == "t":
                    p, j = divmod(u[1], NJ)
                    pe.wait_ge(S["xnT_lo_ok"], p + 1)
                    pe.wait_ge(S["A_ok"], TH * j // GH + 1)
                    for h in range(TH):
                        head = TH * j + h
                        last = split_mm(bank[:, h * 2 * T:(h + 1) * 2 * T], A_hi[:, head, :], A_lo[:, head, :],
                                        xnT_hi[:, 2 * p:2 * p + 2, :].rearrange("p b t -> p (b t)"),
                                        xnT_lo[:, 2 * p:2 * p + 2, :].rearrange("p b t -> p (b t)"))
                else:
                    _, b, i = u
                    pe.wait_ge(S["vw_lo_ok"], i + 1)
                    cols = slice(i * VC, (i + 1) * VC)
                    last = split_mm(bank, xnT_hi[:, b, :], xnT_lo[:, b, :], vw_hi[:, cols], vw_lo[:, cols])
                last.then_inc(S["proj_ps"], 1)

            def scores(n):
                b, g = divmod(n, NG)
                pe.wait_ge(S["t_lo_ok"], NJ * (b // 2) + GH * (g + 1) // TH)
                if n >= 2:
                    pe.wait_ge(S["min_ok"], n - 1)
                t = (NJ * (b // 2) + GH * g // TH) % TR
                t_of = [x[:, t:t + GH // TH, :, b % 2, :].rearrange("p a h t -> p (a h) t") for x in (t_hi, t_lo)]
                split_mm(ps[:, SC[n % 2], :], xnT_hi[:, b, :], xnT_lo[:, b, :], *t_of).then_inc(S["s_ps"], 1)

            def transpose_p(n):
                pe.wait_ge(S["pn_ok"], n + 1)
                if n:
                    pe.wait_ge(S["pt_ok"], n)
                else:
                    pe.wait_ge(S["A_ok"], A_BANK.index(PT) + 1)
                for j in range(GH):
                    last = nc.tensor.transpose(ps[:, PT, j * T:(j + 1) * T], p_sb[:, n % 4, j, :],
                                               ident[:, :])
                last.then_inc(S["pt_ps"], 1)

            def attend(n):
                b, g = divmod(n, NG)
                pe.wait_ge(S["pt_ok"], n + 1)
                pe.wait_ge(S["proj_ok"], TURN["v", b, NV - 1] + 1)
                if n == 0:
                    pe.wait_ge(S["A_ok"], A_BANK.index(YB) + 1)
                elif n % 2 == 0:
                    pe.wait_ge(S["y_ok"], n // 2)
                for j in range(GH):
                    col = ((n % 2) * 2 + j // 2) * T
                    r = (j % 2) * DV
                    last = mm(ps[r:r + DV, YB, col:col + T], v_sb[:, b % 2, GH * g + j, :],
                              pT_sb[:, n % 2, j, :], start=True, stop=True)
                last.then_inc(S["y_ps"], 1)

            def context(n, place):
                i = PRE.get(4 * n + place, -1)
                k, h = divmod(i, 2)
                if 0 <= i < 8:
                    if i == 0:
                        pe.wait_ge(S["ctx_in"], 16)
                        pe.wait_ge(S["small_in"], 16 * 7)
                        pe.wait_ge(S["A_ok"], NG)
                    if k == 2:
                        pe.wait_ge(S["pre_ok"], 2)
                        pe.wait_ge(S["wq_ok"], 1)
                    if k == 3:
                        pe.wait_ge(S["bq_ok"], 1)
                    if i >= 2:
                        pe.wait_ge(S["pre_ok"], i - 1)
                    w, src = ((wkT_sb, ctxT_sb), (wvT_sb, ctxT_sb), (wq_sb, kpT), (bq_bc, kpT))[k]
                    mm(ps[:, MB[h], 0:HALF], w[:, :], src[:, h * HALF:(h + 1) * HALF],
                       start=True, stop=True).then_inc(S["pre_ps"], 1)
                elif 8 <= i < 10:
                    pe.wait_ge(S["pre_ok"], i - 1)
                    for j in range(4):
                        b = 4 * h + j
                        last = mm(ps[0:S2, MB[h], j * D:(j + 1) * D], vpT[:, b * S2:(b + 1) * S2], woT_sb[:, :],
                                  start=True, stop=True)
                    last.then_inc(S["vo_ps"], 1)
                elif i == 10:
                    pe.wait_ge(S["vo_ok"], 1)
                    pe.wait_ge(S["gate_in"], 32)
                    pe.wait_ge(S["consts_ok"], 2)
                    mm(ps[:, MB[0], 0:E], centre[:, :], gw_sb[:, :], start=True, stop=True) \
                        .then_inc(S["gw_ps"], 1)

            def chain(n, place):
                for b, k in chain_at(n, place, ("za", "z", "tr2", "sc2", "trp2", "o2", "tr3", "lg", "pf")):
                    chain_step(b, k)

            def chain_step(b, k):
                m = MB[b % 2]
                if k in ("za", "z"):
                    first = k == "za"
                    pe.wait_ge(S["y_ok"], 2 * b + (1 if first else 2))
                    if first:
                        pe.wait_ge(S["vo_ok"], 2)
                        pe.wait_ge(S["gw_ok"], 1)
                        if b >= 2:
                            pe.wait_ge(S["slot_ok"], b - 1)
                    for p in range(0 if first else NP // 2, NP // 2 if first else NP):
                        last = mm(ps[:, m, 0:D], yT_sb[:, b % 2, p, :], ww_sb[:, p, :],
                                  start=(p == 0), stop=(p == NP - 1))
                    last.then_inc(S["za_ps" if first else "z_ps"], 1)
                elif k == "tr2":
                    pe.wait_ge(S["x1_ok"], b + 1)
                    nc.tensor.transpose(ps[:, m, 0:T], x1[:, b % 2, :], ident[:, :]).then_inc(S["x1T_ps"], 1)
                elif k == "sc2":
                    pe.wait_ge(S["x1T_ok"], b + 1)
                    mm(ps[:, m, 0:S2], x1T[:, :], qk2[:, b * S2:(b + 1) * S2],
                       start=True, stop=True).then_inc(S["s2_ps"], 1)
                elif k == "trp2":
                    pe.wait_ge(S["p2_ok"], b + 1)
                    nc.tensor.transpose(ps[0:S2, m, 0:T], p2[:, :], ident[:, :]).then_inc(S["p2T_ps"], 1)
                elif k == "o2":
                    pe.wait_ge(S["p2T_ok"], b + 1)
                    mm(ps[:, m, 0:D], p2T[:, :], vo[:, b, :], start=True, stop=True).then_inc(S["o2_ps"], 1)
                elif k == "tr3":
                    pe.wait_ge(S["x2_ok"], b + 1)
                    nc.tensor.transpose(ps[:, m, 0:T], x2[:, b, :], ident[:, :]).then_inc(S["x2T_ps"], 1)
                elif k == "lg":
                    pe.wait_ge(S["x2T_ok"], b + 1)
                    mm(ps[:, m, 0:E], x2T[:, :], gw_centred[:, :], start=True, stop=True) \
                        .then_inc(S["lg_ps"], 1)
                elif k == "pf":
                    pe.wait_ge(S["oh_ok"], b + 1)
                    if b:
                        pe.wait_ge(S["taken_ok"], b)
                    mm(ps[:, m, 0:2 * E], before[:, :], oh[:, :, :].rearrange("p k e -> p (k e)"),
                       start=True, stop=False)
                    mm(ps[:, m, 0:2 * E], ones_b[:, :], taken[:, :, :].rearrange("p k e -> p (k e)"),
                       start=False, stop=True).then_inc(S["pf_ps"], 1)

            pe.wait_ge(S["consts_ok"], 1)
            for i in range(WARM[0]):
                mm(ps[:, SC[0], 0:P], ident[:, :], ident[:, :], start=True, stop=True)
            project(("x", 0))
            fold(0)
            fold(1)
            project(("t", 0))
            project(("t", 1))
            for n in STEPS:
                chain(n, 0)
                context(n, 0)
                if 0 <= n + 1 < G:
                    scores(n + 1)
                for u in projections(n):
                    project(u)
                chain(n, 1)
                context(n, 1)
                if 0 <= n - 1 < G:
                    transpose_p(n - 1)
                chain(n, 2)
                context(n, 2)
                if 0 <= n - 2 < G:
                    attend(n - 2)
                chain(n, 3)
                context(n, 3)

            def dispatch(e):
                pe.wait_ge(rows_in[e], 16)
                if e:
                    pe.wait_ge(S["dT_ok"], e)
                for i in range(NT):
                    last = nc.tensor.transpose(ps[:, DT, i * TILE:(i + 1) * TILE], dsp[0:TILE, e, i, 0:D],
                                               ident[0:TILE, 0:TILE])
                last.then_inc(S["dT_ps"], 1)

            def down(i):
                e, f = divmod(i, FC)
                pe.wait_ge(S["h_lo_ok"], i + 1)
                if f == 0 and e >= 2:
                    pe.wait_ge(S["oT_ok"], e - 1)
                cols = slice(f * D, (f + 1) * D)
                last = split_mm(ps[:, OT[e % 2], 0:SLOTS], split_w(0, e, 2)[:, cols], split_w(1, e, 2)[:, cols],
                                hT_hi[:, e % 2, f, :], hT_lo[:, e % 2, f, :],
                                start=(f == 0), stop=(f == FC - 1))
                if f == FC - 1:
                    last.then_inc(S["oT_ps"], 1)

            def by_row(e):
                pe.wait_ge(S["oT_ok"], e + 1)
                if e:
                    pe.wait_ge(S["eo_ok"], NT * e)
                for i in range(NT):
                    last = nc.tensor.transpose(ps[0:TILE, OUT_B, i * D:(i + 1) * D],
                                               oT[:, i * TILE:(i + 1) * TILE],
                                               ident[:, :])
                last.then_inc(S["o_ps"], 1)

            pe.wait_ge(S["w_hi_ok"], 3)
            for i in range(WARM[1]):
                mm(ps[:, PT, :], split_w(0, 0, 0)[:, 0:P], split_w(0, 0, 0), start=True, stop=True)
            dispatch(0)
            for i in range((E + 2) * FC):
                e, f = divmod(i, FC)
                if e < E:
                    if f == 0:
                        pe.wait_ge(S["dT_ok"], e + 1)
                        pe.wait_ge(S["w_lo_ok"], 3 * (e + 1))
                    if i >= 2:
                        pe.wait_ge(S["h_ok"], i - 1)
                    cols = slice(f * P, (f + 1) * P)
                    split_mm(ps[:, GATE[i % 2], 0:SLOTS], split_w(0, e, 0)[:, cols], split_w(1, e, 0)[:, cols],
                             dT_hi[:, e % 2, :], dT_lo[:, e % 2, :]).then_inc(S["g_ps"], 1)
                    split_mm(ps[:, UP[i % 2], 0:SLOTS], split_w(0, e, 1)[:, cols], split_w(1, e, 1)[:, cols],
                             dT_hi[:, e % 2, :], dT_lo[:, e % 2, :]).then_inc(S["u_ps"], 1)
                expert_steps(2 * i, (("rows", dispatch), ("by_row", by_row)))
                if 0 <= i - DOWN_LAG < E * FC:
                    down(i - DOWN_LAG)
                expert_steps(2 * i + 1, (("rows", dispatch), ("by_row", by_row)))


def kernel(**inputs):
    import numpy as _np
    import concourse.bacc as _bacc
    from concourse import mybir as _mybir
    from concourse.bass_utils import run_bass_kernel_spmd as _run

    i = {k: _np.asarray(v) for k, v in inputs.items()}
    B, T, D = i["x"].shape
    DQ, _, H = i["L0_attn_Q"].shape
    DV = i["L0_attn_V"].shape[0]
    E, F, _ = i["L0_ffn_wi_gate"].shape

    def halves(w):
        return w.reshape(DQ, D, H // 8, 2, 4).transpose(3, 0, 2, 4, 1).reshape(2 * DQ, H // 2, D)

    arrays = {
        "x": i["x"],
        "ctxT": i["ctx_1024"].reshape(-1, D).T,
        "q_w": halves(i["L0_attn_Q"]),
        "k_w": halves(i["L0_attn_K"]),
        "v_w": i["L0_attn_V"].transpose(1, 2, 0).reshape(D, H * DV),
        "w_w": i["L0_attn_W"].reshape(D, DV, H // 2, 2).transpose(3, 1, 2, 0).reshape(2 * DV, H // 2, D),
        "wkT": i["L0_xattn_Wk"].T,
        "wvT": i["L0_xattn_Wv"].T,
        "bv": i["L0_xattn_bv"],
        "wq": i["L0_xattn_Wq"],
        "bq": i["L0_xattn_bq"],
        "woT": i["L0_xattn_Wo"].T,
        "bo": i["L0_xattn_bo"],
        "gate_wT": i["L0_ffn_gate_w"].T,
        "wgT": i["L0_ffn_wi_gate"].transpose(2, 0, 1),
        "wuT": i["L0_ffn_wi_up"].transpose(2, 0, 1),
        "wdT": i["L0_ffn_wo"].reshape(E, D, F // 128, 128).transpose(3, 0, 2, 1),
    }
    arrays = {k: _np.ascontiguousarray(v) for k, v in arrays.items()}
    nc = _bacc.Bacc("TRN2", target_bir_lowering=False, num_devices=1)
    args = [nc.dram_tensor(k, v.shape, _mybir.dt.from_np(v.dtype), kind="ExternalInput").ap()
            for k, v in arrays.items()]
    out = nc.dram_tensor("out", (B * T + SCRATCH_ROWS, D), _mybir.dt.float32, kind="ExternalOutput").ap()
    decoder_layer(nc, *args, out)
    r = _run(nc, [arrays], core_ids=[0])
    return r.results[0]["out"][:B * T].reshape(B, T, D)
```
